# Optimizing a Trainium2 kernel written in Bass

```python
import numpy as np
import jax
import jax.numpy as jnp

def _softmax(x, axis=-1):
    return jax.nn.softmax(x, axis=axis)

def _gelu(x):
    return jax.nn.gelu(x, approximate=True)

def _silu(x):
    return jax.nn.silu(x)

def _sigmoid(x):
    return jax.nn.sigmoid(x)

def _layernorm(x, axis=-1, eps=1e-05):
    m = jnp.mean(x, axis=axis, keepdims=True)
    v = jnp.var(x, axis=axis, keepdims=True)
    return (x - m) / jnp.sqrt(v + eps)

def _scatter_add(tgt, idx, src, axis=0):
    return tgt.at[idx].add(src)

def _segment_sum(src, seg, n):
    return jax.ops.segment_sum(src, seg, n)
kernel_name = 'mk_early_fusion_embed_d1_tok_img256_r4_d7008b'

def setup_inputs(seed: int=0):
    np.random.seed(seed)
    _w = jnp.asarray

    def _rec_inputs():
        import jax
        import jax.numpy as jnp
        _rk = jax.random.key(seed)
        x = 9.04603e-05 + 1.00016 * jax.random.normal(jax.random.fold_in(_rk, 1), (4, 1, 224, 224), jnp.float32)
        x_txt = jax.random.randint(jax.random.fold_in(_rk, 51), (4, 32), 0, 64, jnp.int32)
        return (x, x_txt)
    x, x_txt = _rec_inputs()

    def _L0_tok_setup():
        import jax, jax.numpy as jnp
        import numpy as np
        WS = 7
        H = W = 56
        C = 64
        NH = 8
        HD = C // NH
        SCALE = HD ** (-0.5)
        SHIFT = WS // 2
        N = WS * WS

        def _rel_pos_index():
            coords = np.stack(np.meshgrid(np.arange(WS), np.arange(WS), indexing='ij'))
            cf = coords.reshape(2, -1)
            rel = (cf[:, :, None] - cf[:, None, :]).transpose(1, 2, 0).copy()
            rel[..., 0] += WS - 1
            rel[..., 1] += WS - 1
            rel[..., 0] *= 2 * WS - 1
            return jnp.array(rel.sum(-1))

        def _attn_mask():
            img = np.zeros((H, W), np.int32)
            cnt = 0
            for h in (slice(0, -WS), slice(-WS, -SHIFT), slice(-SHIFT, None)):
                for w in (slice(0, -WS), slice(-WS, -SHIFT), slice(-SHIFT, None)):
                    cnt += 1
                    img[h, w] = cnt
            mw = img.reshape(H // WS, WS, W // WS, WS).transpose(0, 2, 1, 3).reshape(-1, N)
            diff = mw[:, None, :] - mw[:, :, None]
            return jnp.array(np.where(diff != 0, -100.0, 0.0).astype(np.float32))

        def _layernorm(x, g, b):
            m = x.mean(-1, keepdims=True)
            v = ((x - m) ** 2).mean(-1, keepdims=True)
            return (x - m) * jax.lax.rsqrt(v + 1e-05) * g + b

        def _window_partition(x):
            B = x.shape[0]
            x = x.reshape(B, H // WS, WS, W // WS, WS, C).transpose(0, 1, 3, 2, 4, 5)
            return x.reshape(-1, N, C)

        def _window_reverse(xw, B):
            x = xw.reshape(B, H // WS, W // WS, WS, WS, C).transpose(0, 1, 3, 2, 4, 5)
            return x.reshape(B, H, W, C)

        def _swin_block(x, p, shift, rpi, amask):
            B = x.shape[0]
            shortcut = x
            h = _layernorm(x, p['n1g'], p['n1b']).reshape(B, H, W, C)
            if shift > 0:
                h = jnp.roll(h, (-shift, -shift), axis=(1, 2))
            xw = _window_partition(h)
            B_ = xw.shape[0]
            qkv = (xw @ p['qkv_w'].T + p['qkv_b']).reshape(B_, N, 3, NH, HD).transpose(2, 0, 3, 1, 4)
            q, k, v = (qkv[0], qkv[1], qkv[2])
            attn = jnp.einsum('bhnd,bhmd->bhnm', q * SCALE, k)
            attn = attn + p['rpb'][rpi].transpose(2, 0, 1)[None]
            if shift > 0:
                nW = amask.shape[0]
                attn = attn.reshape(B_ // nW, nW, NH, N, N) + amask[None, :, None]
                attn = attn.reshape(B_, NH, N, N)
            attn = jax.nn.softmax(attn, axis=-1)
            o = jnp.einsum('bhnm,bhmd->bhnd', attn, v).transpose(0, 2, 1, 3).reshape(B_, N, C)
            o = o @ p['proj_w'].T + p['proj_b']
            h = _window_reverse(o, B)
            if shift > 0:
                h = jnp.roll(h, (shift, shift), axis=(1, 2))
            x = shortcut + h.reshape(B, H * W, C)
            y = _layernorm(x, p['n2g'], p['n2b'])
            y = jax.nn.gelu(y @ p['w1'].T + p['b1'], approximate=False)
            return x + y @ p['w2'].T + p['b2']
        key = jax.random.key(seed)
        ks = jax.random.split(key, 8)
        s = 0.02
        return {'x': jax.random.normal(ks[0], (16, 1, 224, 224), jnp.float32), 'pe_w': jax.random.normal(ks[1], (C, 1, 4, 4), jnp.float32) * s, 'pe_b': jnp.zeros((C,), jnp.float32), 'pe_ng': jnp.ones((C,), jnp.float32), 'pe_nb': jnp.zeros((C,), jnp.float32), 'n1g': jnp.ones((2, C), jnp.float32), 'n1b': jnp.zeros((2, C), jnp.float32), 'qkv_w': jax.random.normal(ks[2], (2, 3 * C, C), jnp.float32) * s, 'qkv_b': jnp.zeros((2, 3 * C), jnp.float32), 'rpb': jax.random.normal(ks[3], (2, (2 * WS - 1) ** 2, NH), jnp.float32) * s, 'proj_w': jax.random.normal(ks[4], (2, C, C), jnp.float32) * s, 'proj_b': jnp.zeros((2, C), jnp.float32), 'n2g': jnp.ones((2, C), jnp.float32), 'n2b': jnp.zeros((2, C), jnp.float32), 'w1': jax.random.normal(ks[5], (2, 4 * C, C), jnp.float32) * s, 'b1': jnp.zeros((2, 4 * C), jnp.float32), 'w2': jax.random.normal(ks[6], (2, C, 4 * C), jnp.float32) * s, 'b2': jnp.zeros((2, C), jnp.float32)}
    _L0_tok_all = _L0_tok_setup()
    _L0_tok_in = {k: v for k, v in _L0_tok_all.items() if k in ('pe_w', 'pe_b', 'pe_ng', 'pe_nb', 'n1g', 'n1b', 'qkv_w', 'qkv_b', 'rpb', 'proj_w', 'proj_b', 'n2g', 'n2b', 'w1', 'b1', 'w2', 'b2')}
    del _L0_tok_all

    def _L0_txt_setup():
        import jax, jax.numpy as jnp
        import numpy as np
        V, D, L = (64, 128, 12)
        B, S = (8, 2048)
        EPS = 1e-05

        def layernorm(x, g, b):
            mu = jnp.mean(x, axis=-1, keepdims=True)
            var = jnp.var(x, axis=-1, keepdims=True)
            return (x - mu) * jax.lax.rsqrt(var + EPS) * g + b

        def log_g(x):
            return jnp.where(x >= 0, jnp.log(jax.nn.relu(x) + 0.5), -jax.nn.softplus(-x))

        def heinsen_scan_log(log_coeffs, log_values):
            a_star = jnp.cumsum(log_coeffs, axis=1)
            log_h0_plus_b = jax.lax.cumlogsumexp(log_values - a_star, axis=1)
            return jnp.exp(a_star + log_h0_plus_b)

        def min_gru(x, W):
            hg = x @ W
            hidden, gate = (hg[..., :D], hg[..., D:])
            log_coeffs = -jax.nn.softplus(gate)
            log_z = -jax.nn.softplus(-gate)
            log_values = log_z + log_g(hidden)
            return heinsen_scan_log(log_coeffs, log_values)
        key = jax.random.key(seed)
        k0, k1, k2 = jax.random.split(key, 3)
        tokens = jax.random.randint(k0, (B, S), 0, V)
        emb = jax.random.normal(k1, (V, D), dtype=jnp.float32) * 0.02
        lim = float(np.sqrt(6.0 / (D + 2 * D)))
        W = jax.random.uniform(k2, (L, D, 2 * D), minval=-lim, maxval=lim, dtype=jnp.float32)
        return {'tokens': tokens, 'emb': emb, 'ln_g': jnp.ones((L, D), jnp.float32), 'ln_b': jnp.zeros((L, D), jnp.float32), 'W': W, 'norm_g': jnp.ones((D,), jnp.float32), 'norm_b': jnp.zeros((D,), jnp.float32)}
    _L0_txt_all = _L0_txt_setup()
    _L0_txt_in = {k: v for k, v in _L0_txt_all.items() if k in ('emb', 'ln_g', 'ln_b', 'W', 'norm_g', 'norm_b')}
    del _L0_txt_all

    def _L0_attn_setup():
        import jax, jax.numpy as jnp
        import numpy as np
        from jax import lax
        B_, L_, D_ = (4, 512, 64)
        DI, NS, DC, DTR = (128, 16, 4, 16)
        DFF = 4 * D_

        def _layer_norm(x, g, b, eps=1e-05):
            m = jnp.mean(x, -1, keepdims=True)
            v = jnp.mean((x - m) ** 2, -1, keepdims=True)
            return (x - m) / jnp.sqrt(v + eps) * g + b

        def _mamba(x, in_proj_w, in_proj_b, conv_w, conv_b, x_proj_w, dt_proj_w, dt_proj_b, A_log, D_ssm, out_proj_w, out_proj_b):
            B, L, D = x.shape
            xz = x @ in_proj_w.T + in_proj_b
            xi, z = jnp.split(xz, 2, axis=-1)
            xc = jnp.transpose(xi, (0, 2, 1))
            xc = lax.conv_general_dilated(xc, conv_w[:, None, :], (1,), [(DC - 1, 0)], dimension_numbers=('NCH', 'OIH', 'NCH'), feature_group_count=DI)
            xi = jax.nn.silu(jnp.transpose(xc + conv_b[None, :, None], (0, 2, 1)))
            x_dbl = xi @ x_proj_w.T
            dt, Bs, Cs = jnp.split(x_dbl, [DTR, DTR + NS], axis=-1)
            dt = jax.nn.softplus(dt @ dt_proj_w.T + dt_proj_b)
            A = -jnp.exp(A_log)
            dA = jnp.exp(dt[..., None] * A)
            dBu = dt[..., None] * Bs[:, :, None, :] * xi[..., None]
            dA_t = jnp.moveaxis(dA, 1, 0)
            dBu_t = jnp.moveaxis(dBu, 1, 0)
            C_t = jnp.moveaxis(Cs, 1, 0)

            def step(h, inp):
                a, bu, c = inp
                h = a * h + bu
                y = jnp.einsum('bdn,bn->bd', h, c)
                return (h, y)
            h0 = jnp.zeros((B, DI, NS), x.dtype)
            _, ys = lax.scan(step, h0, (dA_t, dBu_t, C_t))
            y = jnp.moveaxis(ys, 0, 1) + xi * D_ssm
            y = y * jax.nn.silu(z)
            return y @ out_proj_w.T + out_proj_b
        key = jax.random.key(seed)
        ks = jax.random.split(key, 20)
        rn = lambda k, s, sc=0.02: jax.random.normal(k, s, jnp.float32) * sc
        return {'x': jax.random.normal(ks[0], (B_, L_, D_), jnp.float32), 'in_proj_w': rn(ks[1], (2 * DI, D_)), 'in_proj_b': jnp.zeros((2 * DI,), jnp.float32), 'conv_w': rn(ks[2], (DI, DC), 0.1), 'conv_b': jnp.zeros((DI,), jnp.float32), 'x_proj_w': rn(ks[3], (DTR + 2 * NS, DI)), 'dt_proj_w': rn(ks[4], (DI, DTR), 0.1), 'dt_proj_b': rn(ks[5], (DI,), 0.5), 'A_log': jnp.log(jnp.tile(jnp.arange(1, NS + 1, dtype=jnp.float32), (DI, 1))), 'D_ssm': jnp.ones((DI,), jnp.float32), 'out_proj_w': rn(ks[6], (D_, DI)), 'out_proj_b': jnp.zeros((D_,), jnp.float32), 'ln1_g': jnp.ones((D_,), jnp.float32), 'ln1_b': jnp.zeros((D_,), jnp.float32), 'fc1_w': rn(ks[7], (DFF, D_)), 'fc1_b': jnp.zeros((DFF,), jnp.float32), 'fc2_w': rn(ks[8], (D_, DFF)), 'fc2_b': jnp.zeros((D_,), jnp.float32), 'ln2_g': jnp.ones((D_,), jnp.float32), 'ln2_b': jnp.zeros((D_,), jnp.float32)}
    _L0_attn_all = _L0_attn_setup()
    _L0_attn_in = {k: v for k, v in _L0_attn_all.items() if k in ('in_proj_w', 'in_proj_b', 'conv_w', 'conv_b', 'x_proj_w', 'dt_proj_w', 'dt_proj_b', 'A_log', 'D_ssm', 'out_proj_w', 'out_proj_b', 'ln1_g', 'ln1_b', 'fc1_w', 'fc1_b', 'fc2_w', 'fc2_b', 'ln2_g', 'ln2_b')}
    del _L0_attn_all

    def _L0_ffn_setup():
        import jax, jax.numpy as jnp
        import numpy as np
        B, S, D, E, H, K = (4, 1024, 64, 8, 128, 2)
        key = jax.random.key(seed)
        ks = jax.random.split(key, 6)
        x = jax.random.normal(ks[0], (B, S, D), jnp.float32)
        Wg = jax.random.normal(ks[1], (D, E), jnp.float32) * 0.02
        bg = jnp.zeros((E,), jnp.float32)
        W1 = jax.random.normal(ks[2], (E, D, H), jnp.float32) * 0.02
        b1 = jnp.zeros((E, H), jnp.float32)
        W2 = jax.random.normal(ks[3], (E, H, D), jnp.float32) * 0.02
        b2 = jnp.zeros((E, D), jnp.float32)
        return {'x': x, 'Wg': Wg, 'bg': bg, 'W1': W1, 'b1': b1, 'W2': W2, 'b2': b2}
    _L0_ffn_all = _L0_ffn_setup()
    _L0_ffn_in = {k: v for k, v in _L0_ffn_all.items() if k in ('Wg', 'bg', 'W1', 'b1', 'W2', 'b2')}
    del _L0_ffn_all
    return {'x': x, 'x_txt': x_txt, 'L0_tok_pe_w': _L0_tok_in['pe_w'], 'L0_tok_pe_b': _L0_tok_in['pe_b'], 'L0_tok_pe_ng': _L0_tok_in['pe_ng'], 'L0_tok_pe_nb': _L0_tok_in['pe_nb'], 'L0_tok_n1g': _L0_tok_in['n1g'], 'L0_tok_n1b': _L0_tok_in['n1b'], 'L0_tok_qkv_w': _L0_tok_in['qkv_w'], 'L0_tok_qkv_b': _L0_tok_in['qkv_b'], 'L0_tok_rpb': _L0_tok_in['rpb'], 'L0_tok_proj_w': _L0_tok_in['proj_w'], 'L0_tok_proj_b': _L0_tok_in['proj_b'], 'L0_tok_n2g': _L0_tok_in['n2g'], 'L0_tok_n2b': _L0_tok_in['n2b'], 'L0_tok_w1': _L0_tok_in['w1'], 'L0_tok_b1': _L0_tok_in['b1'], 'L0_tok_w2': _L0_tok_in['w2'], 'L0_tok_b2': _L0_tok_in['b2'], 'L0_txt_emb': _L0_txt_in['emb'], 'L0_txt_ln_g': _L0_txt_in['ln_g'], 'L0_txt_ln_b': _L0_txt_in['ln_b'], 'L0_txt_W': _L0_txt_in['W'], 'L0_txt_norm_g': _L0_txt_in['norm_g'], 'L0_txt_norm_b': _L0_txt_in['norm_b'], 'L0_attn_in_proj_w': _L0_attn_in['in_proj_w'], 'L0_attn_in_proj_b': _L0_attn_in['in_proj_b'], 'L0_attn_conv_w': _L0_attn_in['conv_w'], 'L0_attn_conv_b': _L0_attn_in['conv_b'], 'L0_attn_x_proj_w': _L0_attn_in['x_proj_w'], 'L0_attn_dt_proj_w': _L0_attn_in['dt_proj_w'], 'L0_attn_dt_proj_b': _L0_attn_in['dt_proj_b'], 'L0_attn_A_log': _L0_attn_in['A_log'], 'L0_attn_D_ssm': _L0_attn_in['D_ssm'], 'L0_attn_out_proj_w': _L0_attn_in['out_proj_w'], 'L0_attn_out_proj_b': _L0_attn_in['out_proj_b'], 'L0_attn_ln1_g': _L0_attn_in['ln1_g'], 'L0_attn_ln1_b': _L0_attn_in['ln1_b'], 'L0_attn_fc1_w': _L0_attn_in['fc1_w'], 'L0_attn_fc1_b': _L0_attn_in['fc1_b'], 'L0_attn_fc2_w': _L0_attn_in['fc2_w'], 'L0_attn_fc2_b': _L0_attn_in['fc2_b'], 'L0_attn_ln2_g': _L0_attn_in['ln2_g'], 'L0_attn_ln2_b': _L0_attn_in['ln2_b'], 'L0_ffn_Wg': _L0_ffn_in['Wg'], 'L0_ffn_bg': _L0_ffn_in['bg'], 'L0_ffn_W1': _L0_ffn_in['W1'], 'L0_ffn_b1': _L0_ffn_in['b1'], 'L0_ffn_W2': _L0_ffn_in['W2'], 'L0_ffn_b2': _L0_ffn_in['b2']}

def reference(x, x_txt, L0_tok_pe_w, L0_tok_pe_b, L0_tok_pe_ng, L0_tok_pe_nb, L0_tok_n1g, L0_tok_n1b, L0_tok_qkv_w, L0_tok_qkv_b, L0_tok_rpb, L0_tok_proj_w, L0_tok_proj_b, L0_tok_n2g, L0_tok_n2b, L0_tok_w1, L0_tok_b1, L0_tok_w2, L0_tok_b2, L0_txt_emb, L0_txt_ln_g, L0_txt_ln_b, L0_txt_W, L0_txt_norm_g, L0_txt_norm_b, L0_attn_in_proj_w, L0_attn_in_proj_b, L0_attn_conv_w, L0_attn_conv_b, L0_attn_x_proj_w, L0_attn_dt_proj_w, L0_attn_dt_proj_b, L0_attn_A_log, L0_attn_D_ssm, L0_attn_out_proj_w, L0_attn_out_proj_b, L0_attn_ln1_g, L0_attn_ln1_b, L0_attn_fc1_w, L0_attn_fc1_b, L0_attn_fc2_w, L0_attn_fc2_b, L0_attn_ln2_g, L0_attn_ln2_b, L0_ffn_Wg, L0_ffn_bg, L0_ffn_W1, L0_ffn_b1, L0_ffn_W2, L0_ffn_b2):
    import jax
    import jax.numpy as jnp

    def _L0_tok_ref(x, pe_w, pe_b, pe_ng, pe_nb, n1g, n1b, qkv_w, qkv_b, rpb, proj_w, proj_b, n2g, n2b, w1, b1, w2, b2):
        import jax, jax.numpy as jnp
        import numpy as np
        WS = 7
        H = W = 56
        C = 64
        NH = 8
        HD = C // NH
        SCALE = HD ** (-0.5)
        SHIFT = WS // 2
        N = WS * WS

        def _rel_pos_index():
            coords = np.stack(np.meshgrid(np.arange(WS), np.arange(WS), indexing='ij'))
            cf = coords.reshape(2, -1)
            rel = (cf[:, :, None] - cf[:, None, :]).transpose(1, 2, 0).copy()
            rel[..., 0] += WS - 1
            rel[..., 1] += WS - 1
            rel[..., 0] *= 2 * WS - 1
            return jnp.array(rel.sum(-1))

        def _attn_mask():
            img = np.zeros((H, W), np.int32)
            cnt = 0
            for h in (slice(0, -WS), slice(-WS, -SHIFT), slice(-SHIFT, None)):
                for w in (slice(0, -WS), slice(-WS, -SHIFT), slice(-SHIFT, None)):
                    cnt += 1
                    img[h, w] = cnt
            mw = img.reshape(H // WS, WS, W // WS, WS).transpose(0, 2, 1, 3).reshape(-1, N)
            diff = mw[:, None, :] - mw[:, :, None]
            return jnp.array(np.where(diff != 0, -100.0, 0.0).astype(np.float32))

        def _layernorm(x, g, b):
            m = x.mean(-1, keepdims=True)
            v = ((x - m) ** 2).mean(-1, keepdims=True)
            return (x - m) * jax.lax.rsqrt(v + 1e-05) * g + b

        def _window_partition(x):
            B = x.shape[0]
            x = x.reshape(B, H // WS, WS, W // WS, WS, C).transpose(0, 1, 3, 2, 4, 5)
            return x.reshape(-1, N, C)

        def _window_reverse(xw, B):
            x = xw.reshape(B, H // WS, W // WS, WS, WS, C).transpose(0, 1, 3, 2, 4, 5)
            return x.reshape(B, H, W, C)

        def _swin_block(x, p, shift, rpi, amask):
            B = x.shape[0]
            shortcut = x
            h = _layernorm(x, p['n1g'], p['n1b']).reshape(B, H, W, C)
            if shift > 0:
                h = jnp.roll(h, (-shift, -shift), axis=(1, 2))
            xw = _window_partition(h)
            B_ = xw.shape[0]
            qkv = (xw @ p['qkv_w'].T + p['qkv_b']).reshape(B_, N, 3, NH, HD).transpose(2, 0, 3, 1, 4)
            q, k, v = (qkv[0], qkv[1], qkv[2])
            attn = jnp.einsum('bhnd,bhmd->bhnm', q * SCALE, k)
            attn = attn + p['rpb'][rpi].transpose(2, 0, 1)[None]
            if shift > 0:
                nW = amask.shape[0]
                attn = attn.reshape(B_ // nW, nW, NH, N, N) + amask[None, :, None]
                attn = attn.reshape(B_, NH, N, N)
            attn = jax.nn.softmax(attn, axis=-1)
            o = jnp.einsum('bhnm,bhmd->bhnd', attn, v).transpose(0, 2, 1, 3).reshape(B_, N, C)
            o = o @ p['proj_w'].T + p['proj_b']
            h = _window_reverse(o, B)
            if shift > 0:
                h = jnp.roll(h, (shift, shift), axis=(1, 2))
            x = shortcut + h.reshape(B, H * W, C)
            y = _layernorm(x, p['n2g'], p['n2b'])
            y = jax.nn.gelu(y @ p['w1'].T + p['b1'], approximate=False)
            return x + y @ p['w2'].T + p['b2']
        B = x.shape[0]
        h = jax.lax.conv_general_dilated(x, pe_w, (4, 4), 'VALID', dimension_numbers=('NCHW', 'OIHW', 'NCHW'))
        h = h + pe_b[None, :, None, None]
        t = h.reshape(B, C, H * W).transpose(0, 2, 1)
        t = _layernorm(t, pe_ng, pe_nb)
        rpi = _rel_pos_index()
        amask = _attn_mask()
        for i, shift in enumerate((0, SHIFT)):
            p = {'n1g': n1g[i], 'n1b': n1b[i], 'qkv_w': qkv_w[i], 'qkv_b': qkv_b[i], 'rpb': rpb[i], 'proj_w': proj_w[i], 'proj_b': proj_b[i], 'n2g': n2g[i], 'n2b': n2b[i], 'w1': w1[i], 'b1': b1[i], 'w2': w2[i], 'b2': b2[i]}
            t = _swin_block(t, p, shift, rpi, amask)
        return t

    def _L0_txt_ref(tokens, emb, ln_g, ln_b, W, norm_g, norm_b):
        import jax, jax.numpy as jnp
        import numpy as np
        V, D, L = (64, 128, 12)
        B, S = (8, 2048)
        EPS = 1e-05

        def layernorm(x, g, b):
            mu = jnp.mean(x, axis=-1, keepdims=True)
            var = jnp.var(x, axis=-1, keepdims=True)
            return (x - mu) * jax.lax.rsqrt(var + EPS) * g + b

        def log_g(x):
            return jnp.where(x >= 0, jnp.log(jax.nn.relu(x) + 0.5), -jax.nn.softplus(-x))

        def heinsen_scan_log(log_coeffs, log_values):
            a_star = jnp.cumsum(log_coeffs, axis=1)
            log_h0_plus_b = jax.lax.cumlogsumexp(log_values - a_star, axis=1)
            return jnp.exp(a_star + log_h0_plus_b)

        def min_gru(x, W):
            hg = x @ W
            hidden, gate = (hg[..., :D], hg[..., D:])
            log_coeffs = -jax.nn.softplus(gate)
            log_z = -jax.nn.softplus(-gate)
            log_values = log_z + log_g(hidden)
            return heinsen_scan_log(log_coeffs, log_values)
        x = emb[tokens]
        for i in range(L):
            h = layernorm(x, ln_g[i], ln_b[i])
            x = x + min_gru(h, W[i])
        x = layernorm(x, norm_g, norm_b)
        logits = x @ emb.T
        return logits

    def _L0_attn_ref(x, in_proj_w, in_proj_b, conv_w, conv_b, x_proj_w, dt_proj_w, dt_proj_b, A_log, D_ssm, out_proj_w, out_proj_b, ln1_g, ln1_b, fc1_w, fc1_b, fc2_w, fc2_b, ln2_g, ln2_b):
        import jax, jax.numpy as jnp
        import numpy as np
        from jax import lax
        B_, L_, D_ = (4, 512, 64)
        DI, NS, DC, DTR = (128, 16, 4, 16)
        DFF = 4 * D_

        def _layer_norm(x, g, b, eps=1e-05):
            m = jnp.mean(x, -1, keepdims=True)
            v = jnp.mean((x - m) ** 2, -1, keepdims=True)
            return (x - m) / jnp.sqrt(v + eps) * g + b

        def _mamba(x, in_proj_w, in_proj_b, conv_w, conv_b, x_proj_w, dt_proj_w, dt_proj_b, A_log, D_ssm, out_proj_w, out_proj_b):
            B, L, D = x.shape
            xz = x @ in_proj_w.T + in_proj_b
            xi, z = jnp.split(xz, 2, axis=-1)
            xc = jnp.transpose(xi, (0, 2, 1))
            xc = lax.conv_general_dilated(xc, conv_w[:, None, :], (1,), [(DC - 1, 0)], dimension_numbers=('NCH', 'OIH', 'NCH'), feature_group_count=DI)
            xi = jax.nn.silu(jnp.transpose(xc + conv_b[None, :, None], (0, 2, 1)))
            x_dbl = xi @ x_proj_w.T
            dt, Bs, Cs = jnp.split(x_dbl, [DTR, DTR + NS], axis=-1)
            dt = jax.nn.softplus(dt @ dt_proj_w.T + dt_proj_b)
            A = -jnp.exp(A_log)
            dA = jnp.exp(dt[..., None] * A)
            dBu = dt[..., None] * Bs[:, :, None, :] * xi[..., None]
            dA_t = jnp.moveaxis(dA, 1, 0)
            dBu_t = jnp.moveaxis(dBu, 1, 0)
            C_t = jnp.moveaxis(Cs, 1, 0)

            def step(h, inp):
                a, bu, c = inp
                h = a * h + bu
                y = jnp.einsum('bdn,bn->bd', h, c)
                return (h, y)
            h0 = jnp.zeros((B, DI, NS), x.dtype)
            _, ys = lax.scan(step, h0, (dA_t, dBu_t, C_t))
            y = jnp.moveaxis(ys, 0, 1) + xi * D_ssm
            y = y * jax.nn.silu(z)
            return y @ out_proj_w.T + out_proj_b
        gelu = lambda t: jax.nn.gelu(t, approximate=False)
        ssm = _mamba(x, in_proj_w, in_proj_b, conv_w, conv_b, x_proj_w, dt_proj_w, dt_proj_b, A_log, D_ssm, out_proj_w, out_proj_b)
        y = _layer_norm(x + ssm, ln1_g, ln1_b)
        ffn = gelu(gelu(y @ fc1_w.T + fc1_b) @ fc2_w.T + fc2_b)
        return _layer_norm(y + ffn, ln2_g, ln2_b)

    def _L0_ffn_ref(x, Wg, bg, W1, b1, W2, b2):
        import jax, jax.numpy as jnp
        import numpy as np
        B, S, D, E, H, K = (4, 1024, 64, 8, 128, 2)
        Bv, Sv, Dv = x.shape
        gate_scores = x @ Wg + bg
        _, idx = jax.lax.top_k(gate_scores, K)
        mask = jax.nn.one_hot(idx, E, dtype=x.dtype).sum(axis=-2)
        xf = x.reshape(-1, Dv)
        mf = mask.reshape(-1, E)
        h = jax.nn.gelu(jnp.einsum('td,edh->teh', xf, W1) + b1[None], approximate=False)
        y = jnp.einsum('teh,ehd->ted', h, W2) + b2[None]
        out = jnp.einsum('ted,te->td', y, mf)
        return out.reshape(Bv, Sv, Dv)
    h = _L0_tok_ref(x, L0_tok_pe_w, L0_tok_pe_b, L0_tok_pe_ng, L0_tok_pe_nb, L0_tok_n1g, L0_tok_n1b, L0_tok_qkv_w, L0_tok_qkv_b, L0_tok_rpb, L0_tok_proj_w, L0_tok_proj_b, L0_tok_n2g, L0_tok_n2b, L0_tok_w1, L0_tok_b1, L0_tok_w2, L0_tok_b2)
    h = jnp.concatenate([h, _L0_txt_ref(x_txt, L0_txt_emb, L0_txt_ln_g, L0_txt_ln_b, L0_txt_W, L0_txt_norm_g, L0_txt_norm_b)], axis=1)
    h = h + _L0_attn_ref(_layernorm(h, axis=-1), L0_attn_in_proj_w, L0_attn_in_proj_b, L0_attn_conv_w, L0_attn_conv_b, L0_attn_x_proj_w, L0_attn_dt_proj_w, L0_attn_dt_proj_b, L0_attn_A_log, L0_attn_D_ssm, L0_attn_out_proj_w, L0_attn_out_proj_b, L0_attn_ln1_g, L0_attn_ln1_b, L0_attn_fc1_w, L0_attn_fc1_b, L0_attn_fc2_w, L0_attn_fc2_b, L0_attn_ln2_g, L0_attn_ln2_b)
    h = h + _L0_ffn_ref(_layernorm(h, axis=-1), L0_ffn_Wg, L0_ffn_bg, L0_ffn_W1, L0_ffn_b1, L0_ffn_W2, L0_ffn_b2)
    return h

_drawn_inputs = setup_inputs


def setup_inputs(seed=0):
    import zlib

    import numpy as np

    out = dict(_drawn_inputs(seed))
    spreads = {'L0_tok_pe_b': (0.0, 0.1),
     'L0_tok_pe_ng': (1.0, 0.2),
     'L0_tok_pe_nb': (0.0, 0.1),
     'L0_tok_n1g': (1.0, 0.6),
     'L0_tok_n1b': (0.0, 0.8),
     'L0_tok_qkv_b': (0.0, 0.382),
     'L0_tok_proj_b': (0.0, 0.1),
     'L0_tok_n2g': (1.0, 0.6),
     'L0_tok_n2b': (0.0, 0.8),
     'L0_tok_b1': (0.0, 0.359),
     'L0_tok_b2': (0.0, 0.1),
     'L0_txt_ln_g': (1.0, 0.559),
     'L0_txt_ln_b': (0.0, 0.4),
     'L0_txt_norm_g': (1.0, 0.6),
     'L0_txt_norm_b': (0.0, 0.8),
     'L0_attn_in_proj_b': (0.0, 0.8),
     'L0_attn_conv_b': (0.0, 0.8),
     'L0_attn_D_ssm': (1.0, 0.6),
     'L0_attn_out_proj_b': (0.0, 2.0),
     'L0_attn_ln1_g': (1.0, 0.2),
     'L0_attn_ln1_b': (0.0, 0.1),
     'L0_attn_fc1_b': (0.0, 0.8),
     'L0_attn_fc2_b': (0.0, 0.269),
     'L0_attn_ln2_g': (1.0, 0.2),
     'L0_attn_ln2_b': (0.0, 0.1),
     'L0_ffn_bg': (0.0, 0.1),
     'L0_ffn_b1': (0.0, 0.8),
     'L0_ffn_b2': (0.0, 0.1)}
    factors = {'L0_tok_rpb': 37.602,
     'L0_attn_in_proj_w': 8.0,
     'L0_attn_conv_w': 8.0,
     'L0_attn_x_proj_w': 8.0,
     'L0_attn_dt_proj_w': 8.0,
     'L0_attn_dt_proj_b': 8.0,
     'L0_attn_A_log': 8.0,
     'L0_attn_out_proj_w': 8.0,
     'L0_attn_fc1_w': 7.195,
     'L0_attn_fc2_w': 5.585,
     'L0_ffn_W1': 4.81,
     'L0_ffn_W2': 3.933}
    for name, (base, spread) in spreads.items():
        noise = np.random.default_rng([zlib.crc32(name.encode()), seed]).standard_normal(out[name].shape)
        drawn = base * np.exp(spread * noise) if base else spread * noise
        out[name] = jnp.asarray(drawn.astype(out[name].dtype))
    for name, factor in factors.items():
        out[name] = (out[name] * factor).astype(out[name].dtype)
    return out
```

```python
import concourse.bass as bass
from concourse import mybir
from contextlib import ExitStack

FP32 = mybir.dt.float32
BF16 = mybir.dt.bfloat16
I32 = mybir.dt.int32
ALU = mybir.AluOpType
ACT = mybir.ActivationFunctionType
AX = mybir.AxisListType

P = 128
C = 64
SIDE = 56
IMG = SIDE * SIDE
TXT = 32
L = IMG + TXT
COLS = 2 * L
CH = 396
NCH = COLS // CH
WS = 7
WN = WS * WS
NW = SIDE // WS
ROW = NW * WN
NH = 8
HD = C // NH
SHIFT = WS // 2
EPS = 1e-5
TD = 128
TL = 12
TT = 4 * TXT
DI = 128
NS = 16
DTR = 16
NCB = L // CH
NE = 8

LN_EXP = "natural_log_exp_and_others"


def peeled(eng, n, body):
    body(0)
    if n > 1:
        with eng.Fori(1, n) as i:
            body(i)


CREDIT = 32
COUNTED = (
    "ln_mean ln_centred ln_squared ln_var ln_logged ln_rstd ln_scaled ln_normed ln_added mlp_up mlp_gelu "
    "mlp_down mlp_closed mlp_written pe_mm pe_out at_staged at_k_masked at_resid at_zeroed at_q_mm at_q_out at_k_mm "
    "at_k_out at_v_mm at_v_out at_vt_mm at_vt_out at_scores at_biased at_maxed at_centred at_exped "
    "at_summed at_inverted at_probs at_t_mm at_t_out at_pv at_o_out at_proj at_proj_out tx_step "
    "tx_weights0 tx_weights1 tx_start tx_final mb_in mb_in_out mb_conv mb_act mb_gate mb_conv_step mb_bc "
    "mb_dtr mb_dtr_out mb_dt mb_dt_raw mb_dt_abs mb_dt_exp mb_dt_log mb_dt_done mb_u mb_dt_plus1 "
    "mb_dt_low mb_dt_high mb_dt_copied mb_hi mb_rest mb_mid mb_split mb_cleared mb_b mb_c mb_decay "
    "mb_driven mb_scanned mb_c_out mb_read_dve mb_read_pool mb_y mb_skip mb_gated mb_out mb_out_add "
    "me_score me_score_out me_diff me_tied me_beats me_rank me_picked me_up me_gelu me_each me_masked "
    "me_biased me_down me_added st_copied st_turned st_turned_out st_written0 st_written1 "
).split()


class Core:

    def __init__(self, nc, ctx):
        self.nc, self.ctx, self.sems, self.passes = nc, ctx, {}, {}

    def sem(self, name):
        if name not in self.sems:
            self.sems[name] = self.ctx.enter_context(self.nc.semaphore(name))
        return self.sems[name]

    def count_pass(self, name):
        n = self.passes.get(name, 0)
        self.passes[name] = n + 1
        return n

    def sb(self, ctx, name, shape, dt=FP32):
        return ctx.enter_context(self.nc.sbuf_tensor(name, shape, dt))

    def ps(self, ctx, name, shape, dt=FP32):
        return ctx.enter_context(self.nc.psum_tensor(name, shape, dt))


def load(core, pairs):
    nc, done = core.nc, core.sem("loaded")
    before = core.passes.get("loads", 0)
    core.passes["loads"] = before + len(pairs)
    with nc.Block() as block:
        @block.sync
        def _(sp):
            for dst, src in pairs[0::2]:
                sp.dma_start(dst, src).then_inc(done, 16)
            sp.wait_ge(done, 16 * (before + len(pairs)))

        @block.scalar
        def _(act):
            for dst, src in pairs[1::2]:
                act.dma_start(dst, src).then_inc(done, 16)


def layer_norm(core, src, dst, gamma=None, beta=None, plus=None):
    nc = core.nc
    U = 4
    k = core.count_pass("ln")
    B = k * NCH
    added_before = core.passes.get("ln_added", 0) * NCH
    if plus is not None:
        core.count_pass("ln_added")
    s = core.sem
    mean_mm, centred, squared, var_mm = s("ln_mean"), s("ln_centred"), s("ln_squared"), s("ln_var")
    logged, rstd, scaled, normed, added = s("ln_logged"), s("ln_rstd"), s("ln_scaled"), s("ln_normed"), s("ln_added")
    affine = gamma is not None
    with ExitStack() as ctx:
        xc = core.sb(ctx, f"ln{k}_xc", [P, U, CH])
        sq = core.sb(ctx, f"ln{k}_sq", [P, U, CH])
        lg = core.sb(ctx, f"ln{k}_lg", [P, U, CH])
        rs = core.sb(ctx, f"ln{k}_rs", [P, U, CH])
        sc = core.sb(ctx, f"ln{k}_sc", [P, U, CH]) if affine else None
        out = core.sb(ctx, f"ln{k}_out", [P, U, CH]) if plus is not None else None
        mean = core.ps(ctx, f"ln{k}_mean", [P, U, 512])
        var = core.ps(ctx, f"ln{k}_var", [P, U, 512])

        def cols(t, c):
            return t[:, bass.ds(c * CH, CH)]

        def steps(eng, step):
            for c in range(U):
                step(c, c)
            with eng.Fori(1, NCH // U) as i:
                for j in range(U):
                    step(i * U + j, j)
            for c in range(NCH, NCH + U):
                step(c, c % U)

        def live(c):
            return not isinstance(c, int) or 0 <= c < NCH

        with nc.Block() as block:
            @block.tensor
            def _(pe):
                def step(c, j):
                    if live(c):
                        pe.wait_ge(centred, CREDIT + B + c + 1 - U)
                        pe.matmul(mean[:, j, :CH], core.ones64[:, :], cols(src, c),
                                  start=True, stop=True).then_inc(mean_mm, 1)
                    if live(c - 1):
                        v, jv = c - 1, (j - 1) % U
                        pe.wait_ge(squared, CREDIT + B + v + 1)
                        pe.wait_ge(logged, CREDIT + B + v + 1 - U)
                        pe.matmul(var[:, jv, :CH], core.ones64[:, :], sq[:, jv, :],
                                  start=True, stop=True).then_inc(var_mm, 1)
                steps(pe, step)

            @block.vector
            def _(dve):
                def step(c, j):
                    if live(c):
                        dve.wait_ge(mean_mm, CREDIT + B + c + 1)
                        dve.wait_ge(squared, CREDIT + B + c + 1 - U)
                        dve.wait_ge(scaled, CREDIT + B + c + 1 - U)
                        dve.tensor_tensor(xc[:, j, :], cols(src, c), mean[:, j, :CH],
                                          ALU.subtract).then_inc(centred, 1)
                    if live(c - 3):
                        v, jv = c - 3, (j - 3) % U
                        dve.wait_ge(rstd, CREDIT + B + v + 1)
                        if affine:
                            dve.wait_ge(normed, CREDIT + B + v + 1 - U)
                        dve.tensor_tensor(sc[:, jv, :] if affine else cols(dst, v), xc[:, jv, :],
                                          rs[:, jv, :], ALU.mult).then_inc(scaled, 1)
                    if affine and live(c - 4):
                        v = c - 4
                        dve.wait_ge(scaled, CREDIT + B + v + 1)
                        if plus is not None:
                            dve.wait_ge(added, CREDIT + added_before + v + 1 - U)
                        dve.tensor_scalar(out[:, j, :] if plus is not None else cols(dst, v),
                                          sc[:, j, :], gamma, beta, ALU.mult, ALU.add).then_inc(normed, 1)
                steps(dve, step)
                if not affine:
                    dve.sem_inc(normed, NCH)

            @block.scalar
            def _(act):
                act.preload_act_table_set(LN_EXP)

                def step(c, j):
                    if live(c):
                        act.wait_ge(centred, CREDIT + B + c + 1)
                        act.wait_ge(var_mm, CREDIT + B + c + 1 - U)
                        act.activation(sq[:, j, :], xc[:, j, :], ACT.Square).then_inc(squared, 1)
                    if live(c - 1):
                        v, jv = c - 1, (j - 1) % U
                        act.wait_ge(var_mm, CREDIT + B + v + 1)
                        act.wait_ge(rstd, CREDIT + B + v + 1 - U)
                        act.activation(lg[:, jv, :], var[:, jv, :CH], ACT.Ln, bias=core.eps[:, :]).then_inc(logged, 1)
                    if live(c - 2):
                        v, jv = c - 2, (j - 2) % U
                        act.wait_ge(logged, CREDIT + B + v + 1)
                        act.wait_ge(scaled, CREDIT + B + v + 1 - U)
                        act.activation(rs[:, jv, :], lg[:, jv, :], ACT.Exp, scale=-0.5).then_inc(rstd, 1)
                steps(act, step)

            if plus is not None:
                @block.gpsimd
                def _(pool):
                    def step(c, j):
                        if live(c):
                            pool.wait_ge(normed, CREDIT + B + c + 1)
                            pool.tensor_tensor(cols(plus, c), cols(plus, c), out[:, j, :], ALU.add).then_inc(added, 1)
                    steps(pool, step)


def mlp(core, src, w1, b1, w2, b2, dst, residual, outer_gelu):
    nc = core.nc
    k = core.count_pass("mlp")
    B = k * NCH
    s = core.sem
    up_mm, gelued, down_mm, closed, written = s("mlp_up"), s("mlp_gelu"), s("mlp_down"), s("mlp_closed"), s("mlp_written")
    with ExitStack() as ctx:
        hid = core.sb(ctx, f"mlp{k}_hid", [P, 4, CH])
        out = core.sb(ctx, f"mlp{k}_out", [P, 2, CH])
        up = core.ps(ctx, f"mlp{k}_up", [P, 4, 512])
        down = core.ps(ctx, f"mlp{k}_down", [P, 2, 512])

        def cols(t, i, j):
            return t[:, bass.ds((i * 2 + j) * CH, CH)]

        with nc.Block() as block:
            @block.tensor
            def _(pe):
                def body(i):
                    for j in range(2):
                        c = i * 2 + j

                        def first(h):
                            pe.wait_ge(gelued, CREDIT + 4 * B + c * 4 + h + 1 - 4)
                            pe.matmul(up[:, h, :CH], w1[:, h, :], cols(src, i, j),
                                      start=True, stop=True).then_inc(up_mm, 1)

                        def second(h):
                            pe.wait_ge(gelued, CREDIT + 4 * B + c * 4 + h + 1)
                            if h == 0:
                                pe.wait_ge(closed if outer_gelu else written, CREDIT + (core.closed_before if outer_gelu else B) + c + 1 - 2)
                            m = pe.matmul(down[:, j, :CH], w2[:, h, :], hid[:, h, :],
                                          start=(h == 0), stop=(h == 3))
                            if h == 3:
                                m.then_inc(down_mm, 1)

                        for step, h in ((first, 0), (first, 1), (first, 2), (second, 0),
                                        (first, 3), (second, 1), (second, 2), (second, 3)):
                            step(h)
                peeled(pe, NCH // 2, body)

            @block.scalar
            def _(act):
                act.preload_act_table(ACT.Gelu)

                def body(i):
                    for j in range(2):
                        c = i * 2 + j
                        for h in range(4):
                            act.wait_ge(up_mm, CREDIT + 4 * B + c * 4 + h + 1)
                            act.wait_ge(down_mm, CREDIT + B + c)
                            act.activation(hid[:, h, :], up[:, h, :CH], ACT.Gelu,
                                           bias=b1[:, h:h + 1]).then_inc(gelued, 1)
                        if outer_gelu:
                            act.wait_ge(down_mm, CREDIT + B + c + 1)
                            act.wait_ge(written, CREDIT + B + c + 1 - 2)
                            act.activation(out[:, j, :], down[:, j, :CH], ACT.Gelu, bias=b2).then_inc(closed, 1)
                peeled(act, NCH // 2, body)

            @block.vector
            def _(dve):
                def body(i):
                    for j in range(2):
                        c = i * 2 + j
                        if outer_gelu:
                            dve.wait_ge(closed, CREDIT + core.closed_before + c + 1)
                            dve.tensor_tensor(cols(dst, i, j), cols(residual, i, j), out[:, j, :],
                                              ALU.add).then_inc(written, 1)
                        else:
                            dve.wait_ge(down_mm, CREDIT + B + c + 1)
                            dve.scalar_tensor_tensor(out=cols(dst, i, j), in0=down[:, j, :CH], scalar=b2,
                                                     in1=cols(residual, i, j), op0=ALU.add,
                                                     op1=ALU.add).then_inc(written, 1)
                peeled(dve, NCH // 2, body)
    if outer_gelu:
        core.closed_before += NCH


def patch_embed(core, x, pe_w, pe_b, dst):
    nc = core.nc
    s = core.sem
    pix_in, conv_mm, conv_out = s("pe_pixels"), s("pe_mm"), s("pe_out")
    with ExitStack() as ctx:
        pix = core.sb(ctx, "pe_pix", [8, 2, SIDE, 4 * SIDE])
        acc = core.ps(ctx, "pe_acc", [P, 4, 512])
        with nc.Block() as block:
            @block.sync
            def _(sp):
                for b2 in range(2):
                    for half in range(2):
                        sp.dma_start(pix[4 * half:4 * half + 4, b2],
                                     x[2 * half + b2, 0].rearrange("(i k) w -> k i w", k=4)).then_inc(pix_in, 16)

            @block.tensor
            def _(pe):
                for b2 in range(2):
                    pe.wait_ge(pix_in, 16 * 4)

                    def body(i):
                        for j in range(4):
                            c = b2 * NW + i * 4 + j
                            pe.wait_ge(conv_out, CREDIT + c + 1 - 4)
                            for kw in range(4):
                                m = pe.matmul(acc[:, j, :ROW], pe_w[:, kw, :],
                                              pix[:, b2, bass.ds((i * 4 + j) * WS, WS), kw::4],
                                              start=(kw == 0), stop=(kw == 3))
                            m.then_inc(conv_mm, 1)
                    peeled(pe, NW // 4, body)

            @block.scalar
            def _(act):
                act.preload_act_table_set(LN_EXP)
                for b2 in range(2):
                    def body(i):
                        for j in range(4):
                            c = b2 * NW + i * 4 + j
                            act.wait_ge(conv_mm, CREDIT + c + 1)
                            act.activation(dst[:, bass.ds(b2 * L + (i * 4 + j) * ROW, ROW)], acc[:, j, :ROW],
                                           ACT.Identity, bias=pe_b).then_inc(conv_out, 1)
                    peeled(act, NW // 4, body)


def window_parts(shifted, b2, wh):
    if not shifted:
        return [(wh * WS, WS, 0, 0, NW, 0, 0, WS)]
    if isinstance(wh, int) and wh == NW - 1:
        rows = [(SIDE - (WS - SHIFT), WS - SHIFT, 0), (0, SHIFT, WS - SHIFT)]
    else:
        rows = [(wh * WS + SHIFT, WS, 0)]
    parts = []
    for r0, n, i0 in rows:
        parts.append((r0, n, i0, SHIFT, NW - 1, 0, 0, WS))
        parts.append((r0, n, i0, SIDE - (WS - SHIFT), 1, NW - 1, 0, WS - SHIFT))
        parts.append((r0, n, i0, 0, 1, NW - 1, WS - SHIFT, SHIFT))
    return parts


def image_view(t, b2, part):
    r0, n, _, c0, nw, _, _, width = part
    rows = t[:, bass.ds(r0 * SIDE + b2 * L, n * SIDE)].rearrange("p (i c) -> p i c", c=SIDE)
    return rows[:, :, c0:c0 + nw * width].rearrange("p i (w j) -> p w i j", w=nw)


def window_view(t, part):
    _, n, i0, _, nw, w0, j0, width = part
    v = t.rearrange("p (w i j) -> p w i j", w=NW, i=WS)
    return v[:, w0:w0 + nw, i0:i0 + n, j0:j0 + width]


def attention(core, xn, x, p, shifted):
    nc = core.nc
    blk = core.count_pass("attention")
    BC, BQ = NCH * blk, 4 * NCH * blk
    parts_of_row = 1 if not shifted else 3
    s = core.sem
    staged, resid, zeroed, k_masked = s("at_staged"), s("at_resid"), s("at_zeroed"), s("at_k_masked")
    q_mm, q_out, k_mm, k_out = s("at_q_mm"), s("at_q_out"), s("at_k_mm"), s("at_k_out")
    v_mm, v_out, vt_mm, vt_out = s("at_v_mm"), s("at_v_out"), s("at_vt_mm"), s("at_vt_out")
    s_mm, biased, maxed, centred, exped = s("at_scores"), s("at_biased"), s("at_maxed"), s("at_centred"), s("at_exped")
    summed, inverted, probs = s("at_summed"), s("at_inverted"), s("at_probs")
    t_mm, t_out, pv_mm, o_out, proj_mm, proj_out = (s("at_t_mm"), s("at_t_out"), s("at_pv"), s("at_o_out"),
                                                    s("at_proj"), s("at_proj_out"))
    with ExitStack() as ctx:
        def sb(name, shape, dt=FP32):
            return core.sb(ctx, f"at{blk}_{name}", shape, dt)

        xw = sb("xw", [P, 2, ROW])
        qd = sb("qd", [P, 2, NW, P])
        kf = sb("kf", [P, 2, ROW])
        km = sb("km", [P, 2, NW, NH * WN])
        vf = sb("vf", [P, NW, 2 * WN])
        vb = sb("vb", [2 * WN, 2, NW, 2 * NH // 2, 32])
        e = sb("e", [P, 4, 2, NH * WN])
        mx = sb("mx", [P, 2, 2 * NH])
        sm = sb("sm", [P, 2, 2 * NH])
        rc = sb("rc", [P, 2, 2 * NH])
        pt = sb("pt", [2 * WN, 2, 4 * P])
        oc = sb("oc", [P, 2, ROW])
        po = sb("po", [P, 2, ROW])
        scores = core.ps(ctx, f"at{blk}_scores", [P, 2, 2, 512])
        tp = core.ps(ctx, f"at{blk}_tp", [P, 512])
        op = core.ps(ctx, f"at{blk}_op", [P, 2, 512])
        gp = core.ps(ctx, f"at{blk}_gp", [P, 512])

        def schedule(emit_prep, emit_slot, finish, eng):
            emit_prep(0)

            def rows(k):
                for j in range(2):
                    c = k * 2 + j
                    for q in range(4):
                        emit_slot(k, j, c, q)
            rows(0)
            with eng.Fori(1, NW - 2) as k:
                rows(k)
            rows(NW - 2)
            rows(NW - 1)
            finish()

        def is_first(c):
            return isinstance(c, int) and c == 0

        def is_last(c):
            return isinstance(c, int) and c == NCH - 1

        def two_before(c, q):
            return (c - 1, q + 2) if q < 2 else (c, q - 2)

        with nc.Block() as block:
            @block.gpsimd
            def _(pool):
                def stage(k, j, c):
                    pool.wait_ge(v_mm, CREDIT + BC + c + 1 - 2)
                    for part in window_parts(shifted, j, k):
                        last = pool.tensor_copy(window_view(xw[:, j, :], part), image_view(xn, j, part))
                    last.then_inc(staged, 1)

                def residual(k, j, c):
                    pool.wait_ge(proj_out, CREDIT + BC + c + 1)
                    for part in window_parts(shifted, j, k):
                        v = image_view(x, j, part)
                        last = pool.tensor_tensor(v, v, window_view(po[:, j, :], part), ALU.add)
                    last.then_inc(resid, 1)

                def normalise(g, buf):
                    pool.wait_ge(inverted, CREDIT + BQ + g + 1)
                    pr = e[:, buf].rearrange("p w (h m) -> p (w h) m", m=WN)
                    pool.tensor_tensor(pr, pr, rc[:, buf % 2, :].unsqueeze(2).to_broadcast([P, 2 * NH, WN]),
                                       ALU.mult).then_inc(probs, 1)

                def mask_heads(j, c, q):
                    if q == 0:
                        pool.wait_ge(k_out, CREDIT + BC + c + 1)
                        pool.wait_ge(s_mm, CREDIT + BQ + 4 * (c - 1))
                    shape = [P, 2, NH, WN]
                    pool.tensor_tensor(km[:, j, 2 * q:2 * q + 2, :].rearrange("p w (h m) -> p w h m", m=WN),
                                       kf[:, j, 2 * q * WN:(2 * q + 2) * WN].rearrange("p (w m) -> p w m", m=WN)
                                       .unsqueeze(2).to_broadcast(shape),
                                       core.headmask.unsqueeze(1).unsqueeze(3).to_broadcast(shape),
                                       ALU.mult).then_inc(k_masked, 1)

                def slot(k, j, c, q):
                    if not (is_first(c) and q == 0):
                        normalise(c * 4 + q - 1, (q - 1) % 4)
                    if q == 0 and not is_first(c):
                        mask_heads(j, c, 3)
                    elif q > 0 and not is_last(c):
                        mask_heads(1 - j, c + 1, q - 1)
                    if q == 3 and not is_first(c):
                        residual(k - (1 - j), (j + 1) % 2, c - 1)
                    if q == 1 and not (isinstance(k, int) and k == NW - 1):
                        stage(k + 1, j, c + 2)

                def finish():
                    normalise(NCH * 4 - 1, 3)
                    residual(NW - 1, 1, NCH - 1)

                pool.memset(qd[:, :, :, :], 0.0).then_inc(zeroed, 1)
                pool.memset(vb[:, :, :, :, :], 0.0).then_inc(zeroed, 1)
                def prep(c):
                    stage(0, 0, 0)
                    stage(0, 1, 1)
                    for q in range(4):
                        mask_heads(0, 0, q)

                schedule(prep, slot, finish, pool)

            @block.tensor
            def _(pe):
                def k_product(j, c):
                    pe.wait_ge(staged, CREDIT + BC + c + 1)
                    pe.wait_ge(vt_out, CREDIT + 2 * (BC + c))
                    pe.matmul(gp[:, :ROW], p["wk"], xw[:, j, :], start=True, stop=True).then_inc(k_mm, 1)

                def q_product(j, c):
                    pe.wait_ge(k_out, CREDIT + BC + c + 1)
                    pe.matmul(gp[:, :ROW], p["wq"], xw[:, j, :], start=True, stop=True).then_inc(q_mm, 1)

                def v_product(j, c):
                    pe.wait_ge(q_out, CREDIT + BC + c + 1)
                    pe.matmul(gp[:, :ROW], p["wv"], xw[:, j, :], start=True, stop=True).then_inc(v_mm, 1)

                def v_transposes(c, half_row, before):
                    pe.wait_ge(v_out, CREDIT + BC + c + 1)
                    if half_row:
                        pe.wait_ge(vt_out, CREDIT + 2 * (BC + c) + 1)
                    elif before is not None:
                        pe.wait_ge(proj_out, CREDIT + BC + before + 1)
                    for w in range(4):
                        m = pe.transpose(gp[0:2 * WN, w * P:(w + 1) * P], vf[:, 4 * half_row + w, :],
                                         core.ident[:, :])
                    m.then_inc(vt_mm, 1)

                def score(j, c, q):
                    g = c * 4 + q
                    pe.wait_ge(q_out, CREDIT + BC + c + 1)
                    pe.wait_ge(k_masked, CREDIT + BQ + g + 1)
                    pe.wait_ge(centred, CREDIT + BQ + g + 1 - 2)
                    for w in range(2):
                        m = pe.matmul(scores[:, q % 2, w, :NH * WN], qd[:, j, 2 * q + w, :],
                                      km[:, j, 2 * q + w, :], start=True, stop=True)
                    m.then_inc(s_mm, 1)

                def transposes(c, q, w):
                    g = c * 4 + q
                    pe.wait_ge(probs, CREDIT + BQ + g + 1)
                    pe.wait_ge(t_out, CREDIT + 2 * (BQ + g) + w)
                    for hp in range(4):
                        m = pe.transpose(tp[0:2 * WN, hp * P:(hp + 1) * P],
                                         e[:, q, w, hp * 2 * WN:(hp + 1) * 2 * WN], core.ident[:, :])
                    m.then_inc(t_mm, 1)

                def values(j, c, q):
                    g = c * 4 + q
                    if q == 0:
                        pe.wait_ge(vt_out, CREDIT + 2 * (BC + c + 1))
                        pe.wait_ge(o_out, CREDIT + BC + c)
                    for w in range(2):
                        pe.wait_ge(t_out, CREDIT + 2 * (BQ + g) + w + 1)
                        win = 2 * q + w
                        for hp in range(4):
                            for half in range(2):
                                m = pe.matmul(op[32 * hp:32 * hp + 32, half, win * WN:(win + 1) * WN],
                                              vb[:, j, win, half * 4 + hp, :],
                                              pt[:, w, hp * P + 64 * half:hp * P + 64 * half + WN],
                                              start=True, stop=True)
                        m.then_inc(pv_mm, 1)

                def projection(c, v_row):
                    pe.wait_ge(o_out, CREDIT + BC + c + 1)
                    if v_row is not None:
                        pe.wait_ge(v_out, CREDIT + BC + v_row + 1)
                    else:
                        pe.wait_ge(vt_out, CREDIT + 2 * (BC + NCH))
                    for half in range(2):
                        m = pe.matmul(gp[64 * half:64 * half + 64, :ROW], p["wo"], oc[:, half, :],
                                      start=True, stop=True)
                    m.then_inc(proj_mm, 1)

                def prep(c):
                    pe.wait_ge(zeroed, CREDIT + 2 * (blk + 1))
                    k_product(0, 0)
                    q_product(0, 0)
                    v_product(0, 0)
                    v_transposes(0, 0, None)
                    v_transposes(0, 1, None)

                def slot(k, j, c, q):
                    cb, qb = two_before(c, q)
                    behind = not (is_first(c) and q < 2)
                    jb = j if q >= 2 else 1 - j
                    ahead = not is_last(c)
                    score(j, c, q)
                    if behind:
                        transposes(cb, qb, 0)
                    if q == 0 and not is_first(c):
                        v_transposes(c, 1, None)
                    if ahead:
                        if q == 1:
                            q_product(1 - j, c + 1)
                        elif q == 2:
                            v_product(1 - j, c + 1)
                        elif q == 3:
                            v_transposes(c + 1, 0, None if is_first(c) else c - 1)
                    if behind:
                        transposes(cb, qb, 1)
                        values(jb, cb, qb)
                    if q == 2 and not is_first(c):
                        projection(c - 1, c + 1 if ahead else None)
                    if q == 0 and ahead:
                        k_product(1 - j, c + 1)

                def finish():
                    for q in (2, 3):
                        transposes(NCH - 1, q, 0)
                        transposes(NCH - 1, q, 1)
                        values(1, NCH - 1, q)
                    pe.wait_ge(proj_out, CREDIT + BC + NCH - 1)
                    projection(NCH - 1, None)

                schedule(prep, slot, finish, pe)

            @block.scalar
            def _(act):
                act.preload_act_table_set(LN_EXP)

                def k_copy(j, c):
                    act.wait_ge(k_mm, CREDIT + BC + c + 1)
                    act.wait_ge(k_masked, CREDIT + BQ + 4 * (c - 1))
                    act.activation(kf[:, j, :], gp[:, :ROW], ACT.Identity, bias=p["bk"]).then_inc(k_out, 1)

                def v_copy(c):
                    act.wait_ge(v_mm, CREDIT + BC + c + 1)
                    act.wait_ge(vt_mm, CREDIT + 2 * (BC + c))
                    act.activation(vf.rearrange("p w (r m) -> p w r m", r=2),
                                   gp[:, :ROW].rearrange("p (w m) -> p w m", m=WN).unsqueeze(2)
                                   .to_broadcast([P, NW, 2, WN]), ACT.Identity, bias=p["bv"]).then_inc(v_out, 1)

                def exponential(c, q):
                    g = c * 4 + q
                    act.wait_ge(centred, CREDIT + BQ + g + 1)
                    act.activation(e[:, q], e[:, q], ACT.Exp).then_inc(exped, 1)

                def pt_copy(c, q, w):
                    g = c * 4 + q
                    act.wait_ge(t_mm, CREDIT + 2 * (BQ + g) + w + 1)
                    act.wait_ge(pv_mm, CREDIT + 2 * (BQ + g - 1) + w + 1)
                    act.activation(pt[:, w, :], tp[0:2 * WN, :], ACT.Copy).then_inc(t_out, 1)

                def o_copies(c):
                    act.wait_ge(pv_mm, CREDIT + 8 * (BC + c + 1))
                    act.wait_ge(proj_mm, CREDIT + BC + c)
                    for half in range(2):
                        m = act.activation(oc[:, half, :], op[:, half, :ROW], ACT.Copy)
                    m.then_inc(o_out, 1)

                def proj_copy(j, c):
                    act.wait_ge(proj_mm, CREDIT + BC + c + 1)
                    act.wait_ge(resid, CREDIT + BC + c + 1 - 2)
                    act.activation(po[:, j, :], gp[:, :ROW], ACT.Identity, bias=p["bo"]).then_inc(proj_out, 1)

                def prep(c):
                    k_copy(0, 0)
                    v_copy(0)

                def slot(k, j, c, q):
                    cb, qb = two_before(c, q)
                    behind = not (is_first(c) and q < 2)
                    ahead = not is_last(c)
                    if behind:
                        pt_copy(cb, qb, 0)
                        pt_copy(cb, qb, 1)
                    if q == 0 and ahead:
                        k_copy(1 - j, c + 1)
                    if q == 2 and ahead:
                        v_copy(c + 1)
                    exponential(c, q)
                    if q == 1 and not is_first(c):
                        o_copies(c - 1)
                    if q == 2 and not is_first(c):
                        proj_copy(1 - j, c - 1)

                def finish():
                    for q in (2, 3):
                        pt_copy(NCH - 1, q, 0)
                        pt_copy(NCH - 1, q, 1)
                    o_copies(NCH - 1)
                    proj_copy(1, NCH - 1)

                schedule(prep, slot, finish, act)

            @block.vector
            def _(dve):
                def q_copies(j, c):
                    dve.wait_ge(q_mm, CREDIT + BC + c + 1)
                    dve.wait_ge(s_mm, CREDIT + BQ + 4 * (c - 1))
                    for half in range(2):
                        rows = slice(64 * half, 64 * half + 64)
                        m = dve.tensor_scalar(qd[rows, j, :, 64 * half:64 * half + WN],
                                              gp[rows, :ROW].rearrange("p (w n) -> p w n", n=WN),
                                              p["bq"][rows, :], HD ** -0.5, ALU.add, ALU.mult)
                    m.then_inc(q_out, 1)

                def vt_copy(j, c, half_row):
                    dve.wait_ge(vt_mm, CREDIT + 2 * (BC + c) + half_row + 1)
                    dve.wait_ge(pv_mm, CREDIT + 8 * (BC + c - 1))
                    dve.tensor_tensor(vb[:, j, 4 * half_row:4 * half_row + 4, :, 0:2 * HD],
                                      gp[0:2 * WN, :].rearrange("p (w h d) -> p w h d", w=4, d=2 * HD),
                                      core.paritymask.rearrange("p (h d) -> p h d", d=2 * HD).unsqueeze(1)
                                      .to_broadcast([2 * WN, 4, NH, 2 * HD]), ALU.mult).then_inc(vt_out, 1)

                def add_bias(k, c, q):
                    g = c * 4 + q
                    sc = scores[:, q % 2, :, :NH * WN]
                    kind = (3 if isinstance(k, int) and k == NW - 1 else 0) + (1 if q == 3 else 0) if shifted else 0
                    dve.wait_ge(s_mm, CREDIT + BQ + g + 1)
                    dve.tensor_tensor(sc, sc, p["bias"][:, kind:kind + 2, :], ALU.add).then_inc(biased, 1)

                def centre(c, q):
                    g = c * 4 + q
                    sc = scores[:, q % 2, :, :NH * WN]
                    dve.wait_ge(biased, CREDIT + BQ + g + 1)
                    by_head = sc.rearrange("p w (h m) -> p w h m", m=WN)
                    dve.tensor_reduce(mx[:, q % 2, :].rearrange("p (w h) -> p w h", w=2), by_head,
                                      AX.X, ALU.max).then_inc(maxed, 1)
                    dve.wait_ge(maxed, CREDIT + BQ + g + 1)
                    dve.wait_ge(t_mm, CREDIT + 2 * (BQ + g + 1 - 4))
                    dve.tensor_tensor(e[:, q].rearrange("p w (h m) -> p w h m", m=WN), by_head,
                                      mx[:, q % 2, :].rearrange("p (w h) -> p w h", w=2).unsqueeze(3)
                                      .to_broadcast([P, 2, NH, WN]), ALU.subtract).then_inc(centred, 1)

                def total(c, q):
                    g = c * 4 + q
                    dve.wait_ge(exped, CREDIT + BQ + g + 1)
                    dve.tensor_reduce(sm[:, q % 2, :], e[:, q].rearrange("p w (h m) -> p (w h) m", m=WN),
                                      AX.X, ALU.add).then_inc(summed, 1)
                    dve.wait_ge(summed, CREDIT + BQ + g + 1)
                    dve.wait_ge(probs, CREDIT + BQ + g + 1 - 2)
                    dve.reciprocal(rc[:, q % 2, :], sm[:, q % 2, :]).then_inc(inverted, 1)

                def prep(c):
                    dve.wait_ge(zeroed, CREDIT + 2 * (blk + 1))
                    q_copies(0, 0)
                    vt_copy(0, 0, 0)
                    vt_copy(0, 0, 1)

                def slot(k, j, c, q):
                    ahead = not is_last(c)
                    add_bias(k, c, q)
                    if not (is_first(c) and q == 0):
                        total(c if q else c - 1, (q - 1) % 4)
                    if q == 0 and not is_first(c):
                        vt_copy(j, c, 1)
                    centre(c, q)
                    if q == 1 and ahead:
                        q_copies(1 - j, c + 1)
                    if q == 3 and ahead:
                        vt_copy(1 - j, c + 1, 0)

                def finish():
                    total(NCH - 1, 3)

                schedule(prep, slot, finish, dve)


def text_tokens(core, tokens, txt_w, emb_vd, emb_dv, final_gb, logits):
    nc = core.nc
    s = core.sem
    step, weights, tok_in, start, final = s("tx_step"), (s("tx_weights0"), s("tx_weights1")), s("tx_tokens"), s("tx_start"), s("tx_final")
    (MEAN, CENTRE, SQUARE, VAR, LOG, RSTD, SCALE, AFFINE, GATES, EXP, PLUS1, INVERT, RESET, CAND, INPUT, SCAN,
     ADD) = range(1, 18)
    STEPS = ADD
    with ExitStack() as ctx:
        def sb(name, shape, dt=FP32):
            return core.sb(ctx, f"tx_{name}", shape, dt)

        tok_i, tok_f, onehot = sb("tok_i", [64, TT], I32), sb("tok_f", [64, TT]), sb("onehot", [64, TT])
        w = sb("w", [P, 2, 2 * TD + 2])
        x, xc, sq, lg, rs, sc, h = (sb(n, [P, TT]) for n in ("x", "xc", "sq", "lg", "rs", "sc", "h"))
        ex, cand, inp, hs = sb("ex", [P, 3 * TT]), sb("cand", [P, TT]), sb("inp", [P, TT]), sb("hs", [P, TT])
        mean, var = core.ps(ctx, "tx_mean", [P, 512]), core.ps(ctx, "tx_var", [P, 512])
        gates, out = core.ps(ctx, "tx_gates", [P, 512]), core.ps(ctx, "tx_out", [P, 512])

        with nc.Block() as block:
            @block.sync
            def _(sp):
                sp.dma_start(tok_i[:, :], tokens).then_inc(tok_in, 16)

                def body(i):
                    for j in range(2):
                        l = i * 2 + j
                        sp.wait_ge(step, CREDIT + (l - 2) * STEPS + GATES)
                        sp.dma_start(w[:, j, :], txt_w[bass.ds(l, 1)].rearrange("o p n -> p (o n)")).then_inc(weights[j], 16)
                peeled(sp, TL // 2, body)

            @block.tensor
            def _(pe):
                pe.wait_ge(start, CREDIT + 2)
                pe.matmul(out[:, :TT], emb_vd, onehot[:, :], start=True, stop=True).then_inc(start, 1)

                def normal(base):
                    pe.matmul(mean[:, :TT], core.ones128[:, :], x[:, :], start=True, stop=True).then_inc(step, 1)
                    pe.wait_ge(step, CREDIT + base + SQUARE)
                    pe.matmul(var[:, :TT], core.ones128[:, :], sq[:, :], start=True, stop=True).then_inc(step, 1)

                def body(i):
                    for j in range(2):
                        l = i * 2 + j
                        base = l * STEPS
                        pe.wait_ge(step, CREDIT + base)
                        if isinstance(l, int) and l == 0:
                            pe.wait_ge(start, CREDIT + 4)
                        normal(base)
                        pe.wait_ge(weights[j], CREDIT + (i + 1) * 16)
                        pe.wait_ge(step, CREDIT + base + AFFINE)
                        pe.matmul(gates[:, 0:TT], w[:, j, 0:TD], h[:, :], start=True, stop=True)
                        pe.matmul(gates[:, TT:2 * TT], w[:, j, TD:2 * TD], h[:, :], start=True,
                                  stop=True).then_inc(step, 1)
                peeled(pe, TL // 2, body)
                pe.wait_ge(step, CREDIT + TL * STEPS)
                normal(TL * STEPS)
                pe.wait_ge(step, CREDIT + TL * STEPS + AFFINE)
                for half in range(2):
                    m = pe.matmul(out[64 * half:64 * half + 64, :2 * TXT], emb_dv,
                                  h[:, 2 * TXT * half:2 * TXT * half + 2 * TXT], start=True, stop=True)
                m.then_inc(final, 1)

            @block.scalar
            def _(act):
                act.preload_act_table_set(LN_EXP)

                def normal(base):
                    act.wait_ge(step, CREDIT + base + CENTRE)
                    act.activation(sq[:, :], xc[:, :], ACT.Square).then_inc(step, 1)
                    act.wait_ge(step, CREDIT + base + VAR)
                    act.activation(lg[:, :], var[:, :TT], ACT.Ln, bias=core.eps[:, :]).then_inc(step, 1)
                    act.wait_ge(step, CREDIT + base + LOG)
                    act.activation(rs[:, :], lg[:, :], ACT.Exp, scale=-0.5).then_inc(step, 1)

                def body(l):
                    base = l * STEPS
                    normal(base)
                    act.wait_ge(step, CREDIT + base + GATES)
                    act.activation(ex[:, 0:2 * TT], gates[:, 0:2 * TT], ACT.Exp, scale=-1.0)
                    act.activation(ex[:, 2 * TT:3 * TT], gates[:, TT:2 * TT], ACT.Exp).then_inc(step, 1)
                peeled(act, TL, body)
                normal(TL * STEPS)
                act.wait_ge(final, CREDIT + 1)
                act.activation(logits, out[:, :2 * TXT].rearrange("p (b t) -> p b t", t=TXT), ACT.Copy).then_inc(final, 1)

            @block.vector
            def _(dve):
                dve.wait_ge(tok_in, 16)
                dve.tensor_copy(tok_f[:, :], tok_i[:, :]).then_inc(start, 1)
                dve.wait_ge(start, CREDIT + 1)
                dve.tensor_scalar(onehot[:, :], tok_f[:, :], core.iota[0:64, :], None, ALU.is_equal).then_inc(start, 1)
                dve.wait_ge(start, CREDIT + 3)
                dve.tensor_copy(x[:, :], out[:, :TT]).then_inc(start, 1)

                def normal(base, gamma, beta):
                    dve.wait_ge(step, CREDIT + base + MEAN)
                    dve.tensor_tensor(xc[:, :], x[:, :], mean[:, :TT], ALU.subtract).then_inc(step, 1)
                    dve.wait_ge(step, CREDIT + base + RSTD)
                    dve.tensor_tensor(sc[:, :], xc[:, :], rs[:, :], ALU.mult).then_inc(step, 1)
                    dve.wait_ge(step, CREDIT + base + SCALE)
                    dve.tensor_scalar(h[:, :], sc[:, :], gamma, beta, ALU.mult, ALU.add).then_inc(step, 1)

                def body(i):
                    for j in range(2):
                        l = i * 2 + j
                        base = l * STEPS
                        dve.wait_ge(weights[j], CREDIT + (i + 1) * 16)
                        normal(base, w[:, j, 2 * TD:2 * TD + 1], w[:, j, 2 * TD + 1:2 * TD + 2])
                        dve.wait_ge(step, CREDIT + base + EXP)
                        dve.tensor_scalar_add(ex[:, :], ex[:, :], 1.0).then_inc(step, 1)
                        dve.wait_ge(step, CREDIT + base + PLUS1)
                        dve.reciprocal(ex[:, :], ex[:, :]).then_inc(step, 1)
                        dve.wait_ge(step, CREDIT + base + INVERT)
                        dve.memset(ex[:, 2 * TT:3 * TT:TXT], 0.0).then_inc(step, 1)
                        dve.wait_ge(step, CREDIT + base + RESET)
                        dve.scalar_tensor_tensor(out=cand[:, :], in0=gates[:, 0:TT], scalar=0.5, in1=ex[:, 0:TT],
                                                 op0=ALU.add, op1=ALU.max).then_inc(step, 1)
                        dve.wait_ge(step, CREDIT + base + CAND)
                        dve.tensor_tensor(inp[:, :], cand[:, :], ex[:, TT:2 * TT], ALU.mult).then_inc(step, 1)
                        dve.wait_ge(step, CREDIT + base + INPUT)
                        dve.tensor_tensor_scan(hs[:, :], ex[:, 2 * TT:3 * TT], inp[:, :], 0.0, ALU.mult,
                                               ALU.add).then_inc(step, 1)
                        dve.wait_ge(step, CREDIT + base + SCAN)
                        dve.tensor_tensor(x[:, :], x[:, :], hs[:, :], ALU.add).then_inc(step, 1)
                peeled(dve, TL // 2, body)
                normal(TL * STEPS, final_gb[:, 0:1], final_gb[:, 1:2])


def mamba(core, xb, p, spare):
    nc = core.nc
    s = core.sem
    POOL_STATES = tuple(n for n in range(NS) if n % 2 == 0)
    NPOOL = len(POOL_STATES)
    NDVE = NS - NPOOL
    HCB = 8
    CSB = 4 if NPOOL % 4 == 0 else 3 if NPOOL % 3 == 0 else 2
    YLAG = 4
    GATE_AT = min(n for n in POOL_STATES if n >= YLAG - 1)
    OUT_AT = 8
    CBANK = (2, 3, 6, 7)
    (in_mm, in_out, convolved, activated, gate_out) = (s("mb_in"), s("mb_in_out"), s("mb_conv"), s("mb_act"), s("mb_gate"))
    conv_step = s("mb_conv_step")
    (bc_mm, dtr_mm, dtr_out, dt_mm, dt_raw, dt_abs, dt_exp, dt_log, dt_done, u_done) = (
        s("mb_bc"), s("mb_dtr"), s("mb_dtr_out"), s("mb_dt"), s("mb_dt_raw"), s("mb_dt_abs"), s("mb_dt_exp"),
        s("mb_dt_log"), s("mb_dt_done"), s("mb_u"))
    dt_plus1, dt_low, dt_high = s("mb_dt_plus1"), s("mb_dt_low"), s("mb_dt_high")
    dt_copied = s("mb_dt_copied")
    hi_out, rest_out, mid_out, split_out = s("mb_hi"), s("mb_rest"), s("mb_mid"), s("mb_split")
    cleared, b_mm, c_mm, decay, driven, scanned, c_out = (s("mb_cleared"), s("mb_b"), s("mb_c"), s("mb_decay"),
                                                          s("mb_driven"), s("mb_scanned"), s("mb_c_out"))
    read_dve, read_pool, y_mm = s("mb_read_dve"), s("mb_read_pool"), s("mb_y")
    skip, gated, out_mm, out_add = s("mb_skip"), s("mb_gated"), s("mb_out"), s("mb_out_add")
    with ExitStack() as ctx:
        def sb(name, shape, dt=FP32):
            return core.sb(ctx, f"mb_{name}", shape, dt)

        xi = sb("xi", [P, 3 + L])
        u = spare[:, 0:L]
        z = spare[:, L:2 * L]
        dt = xi[:, 3:3 + L]
        du = sb("du", [P, CH])
        bc = sb("bc", [96, L], BF16)
        dtr = sb("dtr", [DTR, 2, CH])
        hi, mid = sb("hi", [96, 2, CH], BF16), sb("mid", [96, 2, CH], BF16)
        rest = sb("rest", [96, 2, CH])
        cv0 = sb("cv", [P, 3, CH])
        da = sb("da", [P, 4, CH])
        hst = sb("hst", [P, NS, CH])
        cv = (cv0, hst[:, 8:11, :])
        raw, ab, ee, ll = ((da[:, n, :], hst[:, n, :]) for n in range(4))
        dr = sb("dr", [P, 2, CH])
        dtc = sb("dtc", [P, CH])
        cs = sb("cs", [P, CSB, CH])
        hc = sb("hc", [P, HCB, CH])
        yt, yg = cv0[:, 0, :], cv0[:, 1, :]
        ps = [core.ps(ctx, f"mb_ps{n}", [P, 512]) for n in range(8)]
        dve_rank = {n: sum(1 for m in range(n) if m not in POOL_STATES) for n in range(NS)}
        pool_rank = {n: sum(1 for m in range(n) if m in POOL_STATES) for n in range(NS)}

        def per_batch(eng, phases):
            with eng.Fori(0, 4) as b:
                for first, body, last in phases:
                    if first is not None:
                        first(b)
                    if last is None:
                        with eng.Fori(0, NCB // 2) as i:
                            body(b, i)
                    else:
                        body(b, 0, b * NCB)
                        with eng.Fori(1, NCB) as i:
                            body(b, i, b * NCB + i)
                        last(b)

        def at(t, i):
            return t[:, bass.ds(i * CH, CH)]

        with nc.Block() as block:
            @block.tensor
            def _(pe):
                def project(b, i):
                    for j in range(2):
                        c = b * NCB + i * 2 + j
                        x_bank, z_bank = (0, 1) if j == 0 else (6, 7)
                        pe.wait_ge(in_out, CREDIT + c - 1)
                        cols = xb[:, bass.ds(b * L + (i * 2 + j) * CH, CH)]
                        pe.matmul(ps[x_bank][:, :CH], p["w_xi"], cols, start=True, stop=True).then_inc(in_mm, 1)
                        pe.wait_ge(gate_out, CREDIT)
                        pe.wait_ge(gate_out, CREDIT + c - 1)
                        pe.matmul(ps[z_bank][:, :CH], p["w_z"], cols, start=True, stop=True).then_inc(in_mm, 1)

                def select(b, i):
                    for j in range(2):
                        c = b * NCB + i * 2 + j
                        pe.wait_ge(gate_out, CREDIT + (b + 1) * NCB)
                        pe.wait_ge(activated, CREDIT + c + 1)
                        pe.wait_ge(rest_out, CREDIT + c - 1)
                        pe.matmul(ps[2 + 3 * j][0:96, :CH], p["w_bc"], at(u, i * 2 + j), start=True,
                                  stop=True).then_inc(bc_mm, 1)
                        pe.wait_ge(dtr_out, CREDIT)
                        pe.wait_ge(dtr_out, CREDIT + c - 1)
                        pe.matmul(ps[3 + 3 * j][0:DTR, :CH], p["w_dtr"], at(u, i * 2 + j), start=True,
                                  stop=True).then_inc(dtr_mm, 1)
                    for j in range(2):
                        c = b * NCB + i * 2 + j
                        pe.wait_ge(dtr_out, CREDIT + c + 1)
                        pe.wait_ge(dt_raw, CREDIT + c - 1)
                        pe.matmul(ps[4 + 3 * j][:, :CH], p["w_dt"], dtr[:, j, :], start=True, stop=True).then_inc(dt_mm, 1)

                def y_sum(c, n):
                    if n in POOL_STATES:
                        pe.wait_ge(read_pool, CREDIT + c * NPOOL + pool_rank[n] + 1)
                    else:
                        pe.wait_ge(read_dve, CREDIT + c * NDVE + dve_rank[n] + 1)
                    if n == 0:
                        pe.wait_ge(skip, CREDIT + c)
                    pe.matmul(ps[4][:, :CH], core.ident[:, :], hc[:, n % HCB, :], start=(n == 0),
                              stop=(n == NS - 1)).then_inc(y_mm, 1)

                def project_out(c):
                    pe.wait_ge(gated, CREDIT + c + 1)
                    pe.wait_ge(out_add, CREDIT + c)
                    pe.matmul(ps[5][0:C, :CH], p["w_out"], yg, start=True, stop=True).then_inc(out_mm, 1)

                def scan(b, i, c):
                    first = isinstance(i, int)
                    if first:
                        pe.wait_ge(split_out, CREDIT + (b + 1) * NCB)
                    for n in range(NS):
                        pe.wait_ge(driven, CREDIT + c * NS + n + 1 - 2)
                        pe.matmul(ps[n % 2][:, :CH], core.select[:, n, :], at(bc, i), start=True,
                                  stop=True).then_inc(b_mm, 1)
                        m = (n - 4) % NS
                        if m in POOL_STATES:
                            pe.wait_ge(c_out, CREDIT + (c - (n < 4)) * NPOOL + pool_rank[m] + 1)
                        else:
                            pe.wait_ge(read_dve, CREDIT + (c - (n < 4)) * NDVE + dve_rank[m] + 1)
                        pe.matmul(ps[CBANK[n % 4]][:, :CH], core.select[:, NS + n, :], at(bc, i), start=True,
                                  stop=True).then_inc(c_mm, 1)
                        if n < YLAG and not first:
                            y_sum(c - 1, NS + n - YLAG)
                        for m in range(NS):
                            if n == max(m + YLAG, YLAG + 2 + m // 2):
                                y_sum(c, m)
                        if n == OUT_AT and not first:
                            project_out(c - 1)

                def scan_last(b):
                    c = b * NCB + NCB - 1
                    for n in range(NS - YLAG, NS):
                        y_sum(c, n)
                    project_out(c)

                per_batch(pe, [(None, project, None), (None, select, None), (None, scan, scan_last)])

            @block.scalar
            def _(act):
                def silu_first(b):
                    act.preload_act_table(ACT.Silu)

                def project(b, i):
                    for j in range(2):
                        c = b * NCB + i * 2 + j
                        act.wait_ge(in_mm, CREDIT + 2 * c + 1)
                        act.activation(xi[:, bass.ds((i * 2 + j) * CH + 3, CH)], ps[0 if j == 0 else 6][:, :CH],
                                       ACT.Identity, bias=p["b_xi"]).then_inc(in_out, 1)
                        act.wait_ge(in_mm, CREDIT + 2 * c + 2)
                        act.activation(at(z, i * 2 + j), ps[1 if j == 0 else 7][:, :CH], ACT.Silu,
                                       bias=p["b_z"]).then_inc(gate_out, 1)
                    for j in range(2):
                        c = b * NCB + i * 2 + j
                        act.wait_ge(convolved, CREDIT + c + 1)
                        act.activation(at(u, i * 2 + j), cv[j][:, 2, :], ACT.Silu, bias=p["b_conv"]).then_inc(activated, 1)

                def exp_first(b):
                    act.preload_act_table_set(LN_EXP)

                def select(b, i):
                    pair = [(j, b * NCB + i * 2 + j) for j in range(2)]
                    for j, c in pair:
                        act.wait_ge(bc_mm, CREDIT + c + 1)
                        act.wait_ge(split_out, CREDIT + c - 1)
                        act.activation(hi[:, j, :], ps[2 + 3 * j][0:96, :CH], ACT.Copy).then_inc(hi_out, 1)
                        act.wait_ge(dtr_mm, CREDIT + c + 1)
                        act.wait_ge(dt_mm, CREDIT + c - 1)
                        act.activation(dtr[:, j, :], ps[3 + 3 * j][0:DTR, :CH], ACT.Copy).then_inc(dtr_out, 1)
                    for j, c in pair:
                        act.wait_ge(rest_out, CREDIT + c + 1)
                        act.activation(mid[:, j, :], rest[:, j, :], ACT.Copy).then_inc(mid_out, 1)
                    for j, c in pair:
                        act.wait_ge(dt_raw, CREDIT + c + 1)
                        act.wait_ge(dt_done, CREDIT + c - 1)
                        act.activation(ab[j], raw[j], ACT.Abs).then_inc(dt_abs, 1)
                    for j, c in pair:
                        act.wait_ge(dt_abs, CREDIT + c + 1)
                        act.activation(ee[j], ab[j], ACT.Exp, scale=-1.0).then_inc(dt_exp, 1)
                    for j, c in pair:
                        act.wait_ge(dt_plus1, CREDIT + c + 1)
                        act.activation(ll[j], ab[j], ACT.Ln).then_inc(dt_log, 1)

                def scan(b, i, c):
                    act.wait_ge(dt_done, CREDIT + (b + 1) * NCB)
                    act.wait_ge(decay, CREDIT + c * NS)
                    act.activation(dtc[:, :], at(dt, i), ACT.Copy).then_inc(dt_copied, 1)
                    act.wait_ge(dt_copied, CREDIT + c + 1)
                    for n in range(NS + 1):
                        if n < NS:
                            act.wait_ge(scanned, CREDIT + c * NS + n + 1 - 4)
                            act.activation(da[:, n % 4, :], dtc[:, :], ACT.Exp, scale=p["A"][:, n:n + 1])\
                                .then_inc(decay, 1)
                        m = n - 1
                        if m in POOL_STATES:
                            r = pool_rank[m]
                            act.wait_ge(c_mm, CREDIT + c * NS + m + 1)
                            act.wait_ge(read_pool, CREDIT + c * NPOOL + r + 1 - CSB)
                            act.activation(cs[:, r % CSB, :], ps[CBANK[m % 4]][:, :CH], ACT.Copy).then_inc(c_out, 1)

                per_batch(act, [(silu_first, project, None), (exp_first, select, None), (None, scan, lambda b: None)])

            @block.vector
            def _(dve):
                def conv_first(b):
                    dve.wait_ge(convolved, CREDIT + b * NCB)
                    dve.wait_ge(gated, CREDIT + b * NCB)
                    dve.wait_ge(out_mm, CREDIT + b * NCB)
                    dve.memset(xi[:, 0:3], 0.0).then_inc(conv_step, 1)

                def project(b, i):
                    base = b + 1 + (b * (NCB // 2) + i) * 6
                    dve.wait_ge(activated, CREDIT + b * NCB + i * 2)
                    for t in range(4):
                        for j in range(2):
                            c = b * NCB + i * 2 + j
                            if t == 0:
                                dve.wait_ge(in_out, CREDIT + c + 1)
                                dve.wait_ge(conv_step, CREDIT + base)
                                dve.tensor_scalar(cv[j][:, 0, :], at(xi, i * 2 + j), p["taps"][:, 0:1], None,
                                                  ALU.mult).then_inc(conv_step, 1)
                                continue
                            dve.wait_ge(conv_step, CREDIT + base + 2 * (t - 1) + j + 1)
                            dve.scalar_tensor_tensor(out=cv[j][:, 2 if t == 3 else t % 2, :],
                                                     in0=xi[:, bass.ds((i * 2 + j) * CH + t, CH)],
                                                     scalar=p["taps"][:, t:t + 1], in1=cv[j][:, (t - 1) % 2, :],
                                                     op0=ALU.mult, op1=ALU.add)\
                                .then_inc(convolved if t == 3 else conv_step, 1)

                def select(b, i):
                    pair = [(j, b * NCB + i * 2 + j) for j in range(2)]
                    for j, c in pair:
                        dve.wait_ge(hi_out, CREDIT + c + 1)
                        dve.wait_ge(mid_out, CREDIT + c - 1)
                        dve.scalar_tensor_tensor(out=rest[:, j, :], in0=hi[:, j, :], scalar=core.part[:, 0:1],
                                                 in1=ps[2 + 3 * j][0:96, :CH], op0=ALU.mult,
                                                 op1=ALU.add).then_inc(rest_out, 1)
                    for j, c in pair:
                        dve.wait_ge(dt_mm, CREDIT + c + 1)
                        dve.wait_ge(dt_abs, CREDIT + c - 1)
                        dve.tensor_scalar(raw[j], ps[4 + 3 * j][:, :CH], p["b_dt"], None, ALU.add).then_inc(dt_raw, 1)
                    for j, c in pair:
                        dve.wait_ge(mid_out, CREDIT + c + 1)
                        dve.scalar_tensor_tensor(out=at(bc, i * 2 + j), in0=mid[:, j, :], scalar=core.part[:, 1:2],
                                                 in1=rest[:, j, :], op0=ALU.mult, op1=ALU.add).then_inc(split_out, 1)
                    for j, c in pair:
                        dve.wait_ge(dt_exp, CREDIT + c + 1)
                        dve.tensor_scalar_add(ab[j], ee[j], 1.0).then_inc(dt_plus1, 1)
                    for j, c in pair:
                        dve.wait_ge(dt_plus1, CREDIT + c + 1)
                        dve.scalar_tensor_tensor(out=ee[j], in0=ab[j], scalar=-1.0, in1=ee[j],
                                                 op0=ALU.add, op1=ALU.subtract).then_inc(dt_low, 1)
                    for j, c in pair:
                        dve.wait_ge(dt_log, CREDIT + c + 1)
                        dve.scalar_tensor_tensor(out=ll[j], in0=raw[j], scalar=0.0, in1=ll[j],
                                                 op0=ALU.max, op1=ALU.add).then_inc(dt_high, 1)
                    for j, c in pair:
                        dve.wait_ge(dt_low, CREDIT + c + 1)
                        dve.wait_ge(dt_high, CREDIT + c + 1)
                        dve.tensor_tensor(at(dt, i * 2 + j), ll[j], ee[j], ALU.subtract).then_inc(dt_done, 1)

                def scan_first(b):
                    dve.wait_ge(read_pool, CREDIT + b * (NCB * NPOOL))
                    dve.wait_ge(dt_done, CREDIT + (b + 1) * NCB)
                    dve.memset(hst[:, :, CH - 1], 0.0).then_inc(cleared, 1)

                def scan(b, i, c):
                    dve.wait_ge(dt_done, CREDIT + (b + 1) * NCB)
                    dve.wait_ge(driven, CREDIT + c * NS)
                    dve.tensor_tensor(du[:, :], at(dt, i), at(u, i), ALU.mult).then_inc(u_done, 1)
                    dve.wait_ge(u_done, CREDIT + c + 1)
                    dve.wait_ge(cleared, CREDIT + b + 1)

                    def drive(n):
                        dve.wait_ge(b_mm, CREDIT + c * NS + n + 1)
                        dve.tensor_tensor(dr[:, n % 2, :], du[:, :], ps[n % 2][:, :CH], ALU.mult).then_inc(driven, 1)

                    def step(n):
                        dve.wait_ge(driven, CREDIT + c * NS + n + 1)
                        dve.wait_ge(decay, CREDIT + c * NS + n + 1)
                        if n in POOL_STATES:
                            dve.wait_ge(read_pool, CREDIT + c * NPOOL + pool_rank[n] + 1 - NPOOL)
                        dve.tensor_tensor_scan(hst[:, n, :], da[:, n % 4, :], dr[:, n % 2, :],
                                               hst[:, n, CH - 1:CH], ALU.mult, ALU.add).then_inc(scanned, 1)

                    def read(n):
                        if n in POOL_STATES:
                            return
                        dve.wait_ge(scanned, CREDIT + c * NS + n + 1)
                        dve.wait_ge(c_mm, CREDIT + c * NS + n + 1)
                        dve.wait_ge(y_mm, CREDIT + c * NS + n + 1 - HCB)
                        dve.tensor_tensor(hc[:, n % HCB, :], hst[:, n, :], ps[CBANK[n % 4]][:, :CH],
                                          ALU.mult).then_inc(read_dve, 1)

                    for n in range(NS + 1):
                        if n < NS:
                            drive(n)
                        if n >= 1:
                            read(n - 1)
                        if n < NS:
                            step(n)
                        if not isinstance(i, int):
                            if n == YLAG - 1:
                                skip_term(i - 1, c - 1)
                            if n == OUT_AT + 1:
                                add_out(b, i - 1, c - 1)

                def skip_term(i, c):
                    dve.wait_ge(y_mm, CREDIT + (c + 1) * NS)
                    dve.scalar_tensor_tensor(out=yt, in0=at(u, i), scalar=p["D"], in1=ps[4][:, :CH],
                                             op0=ALU.mult, op1=ALU.add).then_inc(skip, 1)

                def add_out(b, i, c):
                    dve.wait_ge(out_mm, CREDIT + c + 1)
                    cols = xb[:, bass.ds(b * L + i * CH, CH)]
                    dve.scalar_tensor_tensor(out=cols, in0=ps[5][0:C, :CH], scalar=p["b_out"], in1=cols,
                                             op0=ALU.add, op1=ALU.add).then_inc(out_add, 1)

                def scan_last(b):
                    c = b * NCB + NCB - 1
                    skip_term(NCB - 1, c)
                    add_out(b, NCB - 1, c)

                per_batch(dve, [(conv_first, project, None), (None, select, None), (scan_first, scan, scan_last)])

            @block.gpsimd
            def _(pool):
                def gate(i, c):
                    pool.wait_ge(skip, CREDIT + c + 1)
                    pool.wait_ge(out_mm, CREDIT + c)
                    pool.tensor_tensor(yg, yt, at(z, i), ALU.mult).then_inc(gated, 1)

                def scan(b, i, c):
                    for n in POOL_STATES:
                        r = pool_rank[n]
                        pool.wait_ge(scanned, CREDIT + c * NS + n + 1)
                        pool.wait_ge(c_out, CREDIT + c * NPOOL + r + 1)
                        pool.wait_ge(y_mm, CREDIT + c * NS + n + 1 - HCB)
                        pool.tensor_tensor(hc[:, n % HCB, :], hst[:, n, :], cs[:, r % CSB, :],
                                           ALU.mult).then_inc(read_pool, 1)
                        if n == GATE_AT and not isinstance(i, int):
                            gate(i - 1, c - 1)

                per_batch(pool, [(None, scan, lambda b: gate(NCB - 1, b * NCB + NCB - 1))])


def experts(core, xn, x, p):
    nc = core.nc
    s = core.sem
    (score_mm, score_out, diff_mm, tied, beats, rank_mm, picked) = (
        s("me_score"), s("me_score_out"), s("me_diff"), s("me_tied"), s("me_beats"), s("me_rank"), s("me_picked"))
    up_mm, gelued, each_mm, masked, down_mm, added = (s("me_up"), s("me_gelu"), s("me_each"), s("me_masked"),
                                                      s("me_down"), s("me_added"))
    biased = s("me_biased")
    SUM = (2, 7)
    NU = 2 * NE
    with ExitStack() as ctx:
        def sb(name, shape, dt=FP32):
            return core.sb(ctx, f"me_{name}", shape, dt)

        sc, tie = sb("sc", [2 * NE, CH]), sb("tie", [P, CH])
        bt, pick = sb("bt", [P, 2, CH], BF16), sb("pick", [2 * NE, CH])
        hid, hm = sb("hid", [P, 4, CH]), sb("hm", [P, 4, CH])
        ps = [core.ps(ctx, f"me_ps{n}", [P, 512]) for n in range(8)]

        def at(t, c):
            return t[:, bass.ds(c * CH, CH)]

        def chunks(eng, head, units):
            for stage in range(3):
                head(0, 0, stage)

            def pair(i):
                for j in range(2):
                    c = i * 2 + j
                    units(c, j, lambda stage: head(c + 1, 1 - j, stage) if not (isinstance(c, int) and c == NCH - 1)
                          else None)
            with eng.Fori(0, NCH // 2 - 1) as i:
                pair(i)
            pair(NCH // 2 - 1)

        with nc.Block() as block:
            @block.tensor
            def _(pe):
                def head(c, j, stage):
                    if stage == 0:
                        pe.wait_ge(picked, CREDIT + c)
                        pe.matmul(ps[0][0:2 * NE, :CH], p["wg"], at(xn, c), start=True, stop=True).then_inc(score_mm, 1)
                    elif stage == 1:
                        pe.wait_ge(score_out, CREDIT + c + 1)
                        pe.wait_ge(beats, CREDIT + c)
                        pe.matmul(ps[1][:, :CH], core.pairs, sc[:, :], start=True, stop=True).then_inc(diff_mm, 1)
                    else:
                        pe.wait_ge(beats, CREDIT + c + 1)
                        pe.matmul(ps[0][0:2 * NE, :CH], core.rank_all, bt[:, j, :], start=True,
                                  stop=True).then_inc(rank_mm, 1)

                def units(c, j, next_head):
                    pe.wait_ge(picked, CREDIT + c + 1)
                    pe.wait_ge(added, CREDIT + c - 1)
                    pe.matmul(ps[SUM[j]][:, :CH], p["b2"], pick[:, :], start=True, stop=False).then_inc(biased, 1)
                    for n in range(NU + 2):
                        if n < NU:
                            half, ex = n % 2, n // 2
                            pe.wait_ge(gelued, CREDIT + c * NU + n + 1 - 2)
                            pe.matmul(ps[3 + n % 2][:, :CH], p["w1"][:, ex, half, :], at(xn, c), start=True,
                                      stop=True).then_inc(up_mm, 1)
                            pe.wait_ge(masked, CREDIT + c * NU + n + 1 - 2)
                            pe.matmul(ps[5 + n % 2][:, :CH], core.rank_of[:, half * NE + ex, :], bt[:, j, :],
                                      start=True, stop=True).then_inc(each_mm, 1)
                        if n in (2, 6, 10):
                            next_head(n // 4)
                        if n >= 2:
                            m = n - 2
                            half, ex = m % 2, m // 2
                            pe.wait_ge(masked, CREDIT + c * NU + m + 1)
                            pe.matmul(ps[SUM[j]][:, :CH], p["w2"][:, ex, C * (1 - half):C * (1 - half) + P],
                                      hm[:, m % 4, :], start=False, stop=(m == NU - 1)).then_inc(down_mm, 1)
                chunks(pe, head, units)

            @block.scalar
            def _(act):
                act.preload_act_table(ACT.Gelu)

                def head(c, j, stage):
                    if stage == 0:
                        act.wait_ge(score_mm, CREDIT + c + 1)
                        act.wait_ge(diff_mm, CREDIT + c)
                        act.activation(sc[:, :], ps[0][0:2 * NE, :CH], ACT.Identity, bias=p["bg"]).then_inc(score_out, 1)

                def units(c, j, next_head):
                    for n in range(NU):
                        act.wait_ge(up_mm, CREDIT + c * NU + n + 1)
                        act.wait_ge(masked, CREDIT + c * NU + n + 1 - 4)
                        act.activation(hid[:, n % 4, :], ps[3 + n % 2][:, :CH], ACT.Gelu,
                                       bias=p["b1"][:, n // 2:n // 2 + 1]).then_inc(gelued, 1)
                        if n == 3:
                            next_head(0)
                chunks(act, head, units)

            @block.vector
            def _(dve):
                def head(c, j, stage):
                    if stage == 1:
                        dve.wait_ge(diff_mm, CREDIT + c + 1)
                        dve.wait_ge(each_mm, CREDIT + (c - 1) * NU)
                        dve.tensor_scalar(tie[:, :], ps[1][:, :CH], 0.0, core.tie_wins[:, :], ALU.is_equal,
                                          ALU.mult).then_inc(tied, 1)
                        dve.wait_ge(tied, CREDIT + c + 1)
                        dve.scalar_tensor_tensor(out=bt[:, j, :], in0=ps[1][:, :CH], scalar=0.0, in1=tie[:, :],
                                                 op0=ALU.is_gt, op1=ALU.add).then_inc(beats, 1)
                    elif stage == 2:
                        dve.wait_ge(rank_mm, CREDIT + c + 1)
                        dve.wait_ge(biased, CREDIT + c)
                        dve.tensor_scalar(pick[:, :], ps[0][0:2 * NE, :CH], 2.0, None, ALU.is_lt).then_inc(picked, 1)

                def units(c, j, next_head):
                    for n in range(NU):
                        dve.wait_ge(gelued, CREDIT + c * NU + n + 1)
                        dve.wait_ge(each_mm, CREDIT + c * NU + n + 1)
                        dve.wait_ge(down_mm, CREDIT + c * NU + n + 1 - 4)
                        dve.scalar_tensor_tensor(out=hm[:, n % 4, :], in0=ps[5 + n % 2][:, :CH], scalar=2.0,
                                                 in1=hid[:, n % 4, :], op0=ALU.is_lt,
                                                 op1=ALU.mult).then_inc(masked, 1)
                        if n == 7:
                            next_head(1)
                        if n == 11:
                            next_head(2)
                    dve.wait_ge(down_mm, CREDIT + (c + 1) * NU)
                    dve.tensor_tensor(at(x, c), at(x, c), ps[SUM[j]][:, :CH], ALU.add).then_inc(added, 1)
                chunks(dve, head, units)


def store(core, x, out):
    nc = core.nc
    s = core.sem
    T = CH // 4
    copied, turned, turned_out, written = s("st_copied"), s("st_turned"), s("st_turned_out"), (s("st_written0"), s("st_written1"))
    out_v = out.rearrange("b (c t p) f -> b c p t f", t=4, p=T)
    with ExitStack() as ctx:
        st = core.sb(ctx, "st_in", [P, 2, CH])
        tok = core.sb(ctx, "st_tok", [T, 2, 4, P])
        ps = core.ps(ctx, "st_ps", [P, 2, 512])
        with nc.Block() as block:
            @block.scalar
            def _(act):
                with act.Fori(0, NCH // 2) as i:
                    for j in range(2):
                        c = i * 2 + j
                        act.wait_ge(turned, CREDIT + c + 1 - 2)
                        act.activation(st[:, j, :], x[:, bass.ds(c * CH, CH)], ACT.Copy).then_inc(copied, 1)

            @block.tensor
            def _(pe):
                with pe.Fori(0, NCH // 2) as i:
                    for j in range(2):
                        c = i * 2 + j
                        pe.wait_ge(copied, CREDIT + c + 1)
                        pe.wait_ge(turned_out, CREDIT + c + 1 - 2)
                        for t in range(4):
                            m = pe.transpose(ps[0:T, j, t * P:(t + 1) * P], st[:, j, t * T:(t + 1) * T],
                                             core.ident[:, :])
                        m.then_inc(turned, 1)

            @block.vector
            def _(dve):
                with dve.Fori(0, NCH // 2) as i:
                    for j in range(2):
                        c = i * 2 + j
                        dve.wait_ge(turned, CREDIT + c + 1)
                        dve.wait_ge(written[j], CREDIT + 32 * i)
                        dve.tensor_copy(tok[:, j].rearrange("p t f -> p (t f)"), ps[0:T, j, :]).then_inc(turned_out, 1)

            @block.sync
            def _(sp):
                for b2 in range(2):
                    with sp.Fori(0, NCB // 2) as i:
                        for j in range(2):
                            c = b2 * NCB + i * 2 + j
                            sp.wait_ge(turned_out, CREDIT + c + 1)
                            for half in range(2):
                                sp.dma_start(out_v[2 * half + b2, bass.ds(i * 2 + j, 1)].rearrange("o p t f -> p (o t) f"),
                                             tok[:, j, :, C * half:C * half + C]).then_inc(written[j], 16)
                for j in range(2):
                    sp.wait_ge(written[j], CREDIT + 32 * (NCH // 2))


def build(nc, tiles, ins, out):
    with ExitStack() as life:
        core = Core(nc, life)
        core.closed_before = 0

        def group(ctx, name):
            table = tiles[name]
            width = ins[name].shape[1]
            whole = core.sb(ctx, f"pack_{name}", [P, width])
            got = {}
            for n, (first, rows, shape) in table.items():
                size = 1
                for d in shape:
                    size *= d
                v = whole[0:rows, first:first + size]
                if len(shape) == 2:
                    v = v.rearrange("p (a b) -> p a b", a=shape[0])
                elif len(shape) == 3:
                    v = v.rearrange("p (a b c) -> p a b c", a=shape[0], b=shape[1])
                got[n] = v
            return whole, got

        x = core.sb(life, "x", [P, COLS])
        y = core.sb(life, "y", [P, COLS])
        txt = core.sb(life, "txt_logits", [P, 2, TXT])
        eps_t = core.sb(life, "eps", [P, 1])
        whole, g = group(life, "base")
        load(core, [(whole[:, :], ins["base"])])
        core.ones64, core.ones128, core.ident = g["ones64"], g["ones128"], g["ident"]
        core.headmask, core.iota = g["headmask"], g["iota"]
        core.paritymask = g["paritymask"]
        core.eps = eps_t
        made = core.sem("made")
        with nc.Block() as block:
            @block.sync
            def _(sp):
                for name in COUNTED:
                    sp.sem_inc(core.sem(name), CREDIT)
        with nc.Block() as block:
            @block.vector
            def _(dve):
                dve.memset(eps_t[:, :], EPS).then_inc(made, 1)
                dve.memset(x[:, :], 0.0).then_inc(made, 1)
                dve.memset(y[:, :], 0.0).then_inc(made, 1)

        text_tokens(core, ins["tokens"], ins["txt_w"], g["emb_vd"], g["emb_dv"], g["final_gb"], txt[:, :, :])
        patch_embed(core, ins["x"], g["pe_w"], g["pe_b"], y)
        layer_norm(core, y, x, g["pe_g"], g["pe_nb"])

        for i in range(2):
            with ExitStack() as ctx:
                whole, p = group(ctx, f"swin{i}")
                load(core, [(whole[:, :], ins[f"swin{i}"])])
                bias = core.sb(ctx, f"bias{i}", [P, 6, NH * WN])
                with nc.Block() as block:
                    @block.vector
                    def _(dve):
                        for slot, kind in enumerate((0, 0, 1, 2, 2, 3)):
                            dve.tensor_tensor(bias[:, slot, :].rearrange("p (h m) -> p h m", m=WN),
                                              p["rel"].rearrange("p (h m) -> p h m", m=WN),
                                              g["shiftmask"][:, kind, :].unsqueeze(1).to_broadcast([P, NH, WN]),
                                              ALU.add).then_inc(made, 1)
                p["bias"] = bias
                layer_norm(core, x, y, p["g1"], p["n1"])
                attention(core, y, x, p, i == 1)
                layer_norm(core, x, y, p["g2"], p["n2"])
                mlp(core, y, p["w1"], p["b1"], p["w2"], p["b2"], x, x, False)

        with nc.Block() as block:
            @block.vector
            def _(dve):
                dve.tensor_copy(x[:, :].rearrange("p (b l) -> p b l", l=L)[:, :, IMG:L], txt[:, :, :]).then_inc(made, 1)

        layer_norm(core, x, y)
        with ExitStack() as ctx:
            whole, p = group(ctx, "mamba")
            load(core, [(whole[:, :], ins["mamba"])])
            with ExitStack() as inner:
                xb = core.sb(inner, "xb", [C, 4 * L])
                a_t = core.sb(inner, "a_t", [P, NS])
                core.select = core.sb(inner, "select", [96, 2 * NS, P], BF16)
                core.part = p["part"]
                base = core.passes["loads"]
                core.passes["loads"] += 2
                with nc.Block() as block:
                    @block.sync
                    def _(sp):
                        for half in range(2):
                            sp.dma_start(xb[:, half * COLS:(half + 1) * COLS], y[64 * half:64 * half + 64, :])\
                                .then_inc(core.sem("loaded"), 16)
                        sp.wait_ge(core.sem("loaded"), 16 * (base + 2))

                    @block.scalar
                    def _(act):
                        act.activation(a_t[:, :], p["A_log"], ACT.Exp).then_inc(core.sem("a_exp"), 1)

                    @block.vector
                    def _(dve):
                        dve.tensor_copy(core.select[:, :, :], p["onehot"].unsqueeze(2).to_broadcast([96, 2 * NS, P]))\
                            .then_inc(made, 1)
                        dve.wait_ge(core.sem("a_exp"), 1)
                        dve.tensor_scalar(a_t[:, :], a_t[:, :], -1.0, None, ALU.mult).then_inc(made, 1)
                p["A"] = a_t
                mamba(core, xb, p, y)
                base = core.passes["loads"]
                core.passes["loads"] += 2
                with nc.Block() as block:
                    @block.sync
                    def _(sp):
                        for half in range(2):
                            sp.dma_start(y[64 * half:64 * half + 64, :], xb[:, half * COLS:(half + 1) * COLS])\
                                .then_inc(core.sem("loaded"), 16)
                        sp.wait_ge(core.sem("loaded"), 16 * (base + 2))
            layer_norm(core, y, y, p["ln1_g"], p["ln1_b"])
            mlp(core, y, p["fc1"], p["b_fc1"], p["fc2"], p["b_fc2"], y, y, True)
            layer_norm(core, y, y, p["ln2_g"], p["ln2_b"], plus=x)
        layer_norm(core, x, y)
        with ExitStack() as ctx:
            whole, p = group(ctx, "moe")
            load(core, [(whole[:, :], ins["moe"])])
            core.rank_of = core.sb(ctx, "rank_of", [P, 2 * NE, P], BF16)
            rank_all = core.sb(ctx, "rank_all", [P, 2 * NE], BF16)
            with nc.Block() as block:
                @block.vector
                def _(dve):
                    dve.tensor_copy(rank_all[:, :], p["rank"]).then_inc(made, 1)
                    dve.tensor_copy(core.rank_of[:, :, :], p["rank"].unsqueeze(2).to_broadcast([P, 2 * NE, P]))\
                        .then_inc(made, 1)
            core.rank_all, core.pairs, core.tie_wins = rank_all[:, :], p["pairs"], p["tie_wins"]
            experts(core, y, x, p)
        store(core, x, out)


def _pack(np, arrays):
    width = sum(int(np.prod(a.shape[1:])) for a in arrays.values())
    packed, table, first = np.zeros((P, width), np.float32), {}, 0
    for name, a in arrays.items():
        n = int(np.prod(a.shape[1:]))
        packed[:a.shape[0], first:first + n] = a.reshape(a.shape[0], n)
        table[name] = (first, a.shape[0], tuple(a.shape[1:]))
        first += n
    return packed, table


def _halves(np, w):
    out = np.zeros((P, P), np.float32)
    out[:C, :C] = w
    out[C:, C:] = w
    return out


def _twice(np, v):
    return np.concatenate([v, v]).reshape(P, 1)


def _layout(np, a):
    groups = {}
    eye = np.eye(P, dtype=np.float32)
    z = np.zeros
    base = {"ones64": _halves(np, np.full((C, C), 1.0 / C, np.float32)),
            "ones128": np.full((P, P), 1.0 / P, np.float32), "ident": eye}
    channel = np.arange(P) % C
    base["headmask"] = (channel[:, None] // HD == np.arange(NH)[None, :]).astype(np.float32)
    parity = np.arange(2 * WN) // WN
    base["paritymask"] = (parity[:, None] == (np.arange(P)[None, :] // HD) % 2).astype(np.float32)
    base["iota"] = np.arange(P, dtype=np.float32).reshape(P, 1)
    img = z((SIDE, SIDE), np.int32)
    count = 0
    for h in (slice(0, -WS), slice(-WS, -SHIFT), slice(-SHIFT, None)):
        for w in (slice(0, -WS), slice(-WS, -SHIFT), slice(-SHIFT, None)):
            count += 1
            img[h, w] = count
    mask = z((P, 4, WN), np.float32)
    for kind in range(4):
        wh, ww = (NW - 1) * (kind // 2), (NW - 1) * (kind % 2)
        region = img[wh * WS:wh * WS + WS, ww * WS:ww * WS + WS].reshape(-1)
        m = np.where(region[:, None] != region[None, :], np.float32(-100.0), np.float32(0.0))
        mask[:WN, kind] = m
        mask[C:C + WN, kind] = m
    base["shiftmask"] = mask
    pe_w = z((8, 4, P), np.float32)
    for half in range(2):
        pe_w[4 * half:4 * half + 4, :, C * half:C * half + C] = a["L0_tok_pe_w"][:, 0].transpose(1, 2, 0)
    base["pe_w"] = pe_w
    base["pe_b"], base["pe_g"], base["pe_nb"] = (_twice(np, a["L0_tok_" + n]) for n in ("pe_b", "pe_ng", "pe_nb"))
    base["emb_vd"] = a["L0_txt_emb"]
    base["emb_dv"] = a["L0_txt_emb"].T
    base["final_gb"] = np.stack([a["L0_txt_norm_g"], a["L0_txt_norm_b"]], axis=1)
    groups["base"] = base

    ii, jj = np.arange(WN) // WS, np.arange(WN) % WS
    rel_index = (ii[:, None] - ii[None, :] + WS - 1) * (2 * WS - 1) + jj[:, None] - jj[None, :] + WS - 1
    for i in range(2):
        t = {k: a["L0_tok_" + k][i] for k in ("n1g", "n1b", "qkv_w", "qkv_b", "rpb", "proj_w", "proj_b", "n2g", "n2b",
                                             "w1", "b1", "w2", "b2")}
        p = {}
        for n, name in enumerate("qkv"):
            p["w" + name] = _halves(np, t["qkv_w"][n * C:(n + 1) * C].T)
            p["b" + name] = _twice(np, t["qkv_b"][n * C:(n + 1) * C])
        wo = z((4, 32, C), np.float32)
        wo[:, :2 * HD] = t["proj_w"].T.reshape(4, 2 * HD, C)
        p["wo"], p["bo"] = wo.reshape(P, C), _twice(np, t["proj_b"])
        rel = z((P, NH, WN), np.float32)
        gathered = t["rpb"][rel_index].transpose(0, 2, 1)
        rel[:WN], rel[C:C + WN] = gathered, gathered
        p["rel"] = rel.reshape(P, NH * WN)
        p["g1"], p["n1"], p["g2"], p["n2"] = (_twice(np, t[n]) for n in ("n1g", "n1b", "n2g", "n2b"))
        p.update(_mlp_layout(np, "w1", "b1", "w2", "b2", t["w1"], t["b1"], t["w2"], t["b2"]))
        groups[f"swin{i}"] = p

    m = {k: a["L0_attn_" + k] for k in ("in_proj_w", "in_proj_b", "conv_w", "conv_b", "x_proj_w", "dt_proj_w",
                                        "dt_proj_b", "A_log", "D_ssm", "out_proj_w", "out_proj_b", "ln1_g", "ln1_b",
                                        "fc1_w", "fc1_b", "fc2_w", "fc2_b", "ln2_g", "ln2_b")}
    p = {"w_xi": m["in_proj_w"][:DI].T, "w_z": m["in_proj_w"][DI:].T, "b_xi": m["in_proj_b"][:DI].reshape(P, 1),
         "b_z": m["in_proj_b"][DI:].reshape(P, 1), "taps": m["conv_w"], "b_conv": m["conv_b"].reshape(P, 1),
         "w_dtr": m["x_proj_w"][:DTR].T, "w_bc": np.concatenate([m["x_proj_w"][DTR:].T] * 3, axis=1),
         "w_dt": m["dt_proj_w"].T, "b_dt": m["dt_proj_b"].reshape(P, 1), "A_log": m["A_log"],
         "D": m["D_ssm"].reshape(P, 1), "w_out": m["out_proj_w"].T, "b_out": m["out_proj_b"].reshape(C, 1)}
    p["ln1_g"], p["ln1_b"], p["ln2_g"], p["ln2_b"] = (_twice(np, m[n]) for n in ("ln1_g", "ln1_b", "ln2_g", "ln2_b"))
    p.update(_mlp_layout(np, "fc1", "b_fc1", "fc2", "b_fc2", m["fc1_w"], m["fc1_b"], m["fc2_w"], m["fc2_b"]))
    p["onehot"] = np.concatenate([np.eye(2 * NS, dtype=np.float32)] * 3, axis=0)
    part = z((96, 2), np.float32)
    part[32:, 0] = -1.0
    part[64:, 1] = -1.0
    p["part"] = part
    groups["mamba"] = p

    f = {k: a["L0_ffn_" + k] for k in ("Wg", "bg", "W1", "b1", "W2", "b2")}
    wg = z((P, 2 * NE), np.float32)
    wg[:C, :NE], wg[C:, NE:] = f["Wg"], f["Wg"]
    w1 = z((P, NE, 2, P), np.float32)
    w1[:C, :, 0], w1[C:, :, 1] = f["W1"].transpose(1, 0, 2), f["W1"].transpose(1, 0, 2)
    w2 = z((P, NE, 3 * C), np.float32)
    w2[:, :, C:2 * C] = f["W2"].transpose(1, 0, 2)
    b2 = z((2 * NE, P), np.float32)
    b2[:NE, :C], b2[NE:, C:] = f["b2"], f["b2"]
    pairs = z((2 * NE, 2, NE, NE), np.float32)
    rank = z((2, NE, NE, 2 * NE), np.float32)
    wins = z((2, NE, NE), np.float32)
    for half in range(2):
        for e1 in range(NE):
            for e2 in range(NE):
                if e1 != e2:
                    pairs[half * NE + e2, half, e1, e2] = 1.0
                    pairs[half * NE + e1, half, e1, e2] = -1.0
                    rank[half, e1, e2, half * NE + e1] = 1.0
                wins[half, e1, e2] = float(e2 < e1)
    groups["moe"] = {"wg": wg, "bg": np.concatenate([f["bg"], f["bg"]]).reshape(2 * NE, 1), "w1": w1,
                     "b1": f["b1"].T, "w2": w2, "b2": b2, "pairs": pairs.reshape(2 * NE, P),
                     "rank": rank.reshape(P, 2 * NE), "tie_wins": wins.reshape(P, 1)}
    txt_w = np.concatenate([a["L0_txt_W"], a["L0_txt_ln_g"][:, :, None], a["L0_txt_ln_b"][:, :, None]], axis=2)
    return groups, np.ascontiguousarray(txt_w)


def _mlp_layout(np, n1, nb1, n2, nb2, w1, b1, w2, b2):
    up = np.stack([_halves(np, w1[h * C:(h + 1) * C].T) for h in range(4)], axis=1)
    down = np.stack([_halves(np, w2[:, h * C:(h + 1) * C].T) for h in range(4)], axis=1)
    bias = np.concatenate([b1.reshape(4, C).T] * 2, axis=0)
    return {n1: up, nb1: bias, n2: down, nb2: _twice(np, b2)}


def kernel(**inputs):
    import numpy as np
    import concourse.bacc as bacc
    from concourse.bass_utils import run_bass_kernel_spmd

    a = {k: np.asarray(v) for k, v in inputs.items()}
    groups, txt_w = _layout(np, a)
    nc = bacc.Bacc("TRN2", target_bir_lowering=False, num_devices=1)
    arrays, ins, tiles = {}, {}, {}

    def add(name, array):
        array = np.ascontiguousarray(array)
        arrays[name + "_dram"] = array
        ins[name] = nc.dram_tensor(name + "_dram", array.shape, mybir.dt.from_np(array.dtype),
                                   kind="ExternalInput").ap()

    add("x", a["x"])
    add("tokens", np.broadcast_to(a["x_txt"].reshape(1, TT), (64, TT)))
    add("txt_w", txt_w)
    for name, group in groups.items():
        packed, tiles[name] = _pack(np, group)
        add(name, packed)
    out = nc.dram_tensor("out_dram", (4, L, C), FP32, kind="ExternalOutput").ap()
    build(nc, tiles, ins, out)
    r = run_bass_kernel_spmd(nc, [arrays], core_ids=[0])
    return r.results[0]["out_dram"]
```
